# Optimizing a Trainium2 kernel written in Bass

```python
import numpy as np
import jax
import jax.numpy as jnp

def _softmax(x, axis=-1):
    return jax.nn.softmax(x, axis=axis)

def _gelu(x):
    return jax.nn.gelu(x, approximate=True)

def _silu(x):
    return jax.nn.silu(x)

def _sigmoid(x):
    return jax.nn.sigmoid(x)

def _layernorm(x, axis=-1, eps=1e-05):
    m = jnp.mean(x, axis=axis, keepdims=True)
    v = jnp.var(x, axis=axis, keepdims=True)
    return (x - m) / jnp.sqrt(v + eps)

def _scatter_add(tgt, idx, src, axis=0):
    return tgt.at[idx].add(src)

def _segment_sum(src, seg, n):
    return jax.ops.segment_sum(src, seg, n)
kernel_name = 'mk_adaln_ffn_d1_seqx_r8_6dcb56'

def setup_inputs(seed: int=0):
    np.random.seed(seed)
    _w = jnp.asarray

    def _rec_inputs():
        import jax
        import jax.numpy as jnp
        _rk = jax.random.key(seed)
        x = 7.22e-05 + 1 * jax.random.normal(jax.random.fold_in(_rk, 1), (16, 128, 256), jnp.float32)
        _lenS = 128 - jax.random.randint(jax.random.fold_in(_rk, 7), (16,), 0, max(1, 128 // 4) + 1, jnp.int32)
        _lenS2 = 128 - jax.random.randint(jax.random.fold_in(_rk, 8), (16,), 0, max(1, 128 // 4) + 1, jnp.int32)
        cond_2048 = 0.0061147 + 1.02565 * jax.random.normal(jax.random.fold_in(_rk, 11), (16, 256), jnp.float32)
        return (x, cond_2048)
    x, cond_2048 = _rec_inputs()

    def _L0_cond_setup():
        import jax, jax.numpy as jnp
        import numpy as np
        DIM = 256
        H = 16
        DH = 128
        INNER = H * DH
        MLP = 4 * DIM
        B, T = (2, 256)
        EPS = 1e-06

        def _ln(x):
            mu = jnp.mean(x, axis=-1, keepdims=True)
            var = jnp.var(x, axis=-1, keepdims=True)
            return (x - mu) * jax.lax.rsqrt(var + EPS)
        key = jax.random.key(seed)
        ks = jax.random.split(key, 12)
        s = 0.02
        return {'x': jax.random.normal(ks[0], (B, T, DIM), jnp.float32), 'timestep_embed': jax.random.normal(ks[1], (B, DIM), jnp.float32), 'ada_w': jax.random.normal(ks[2], (DIM, 6 * DIM), jnp.float32) * s, 'ada_b': jnp.zeros((6 * DIM,), jnp.float32), 'qkv_w': jax.random.normal(ks[3], (DIM, 3 * INNER), jnp.float32) * s, 'qkv_b': jnp.zeros((3 * INNER,), jnp.float32), 'out_w': jax.random.normal(ks[4], (INNER, DIM), jnp.float32) * s, 'out_b': jnp.zeros((DIM,), jnp.float32), 'ffn_w1': jax.random.normal(ks[5], (DIM, MLP), jnp.float32) * s, 'ffn_b1': jnp.zeros((MLP,), jnp.float32), 'ffn_w2': jax.random.normal(ks[6], (MLP, DIM), jnp.float32) * s, 'ffn_b2': jnp.zeros((DIM,), jnp.float32)}
    _L0_cond_all = _L0_cond_setup()
    _L0_cond_in = {k: v for k, v in _L0_cond_all.items() if k in ('ada_w', 'ada_b', 'qkv_w', 'qkv_b', 'out_w', 'out_b', 'ffn_w1', 'ffn_b1', 'ffn_w2', 'ffn_b2')}
    del _L0_cond_all

    def _L0_ffn_setup():
        import jax, jax.numpy as jnp
        import numpy as np
        B, S, H = (2, 256, 256)
        E, K = (16, 4)
        I_MOE, I_SH = (176, 704)
        key = jax.random.key(seed)
        ks = jax.random.split(key, 9)

        def w(k, shape, fan_in):
            return jax.random.normal(k, shape, jnp.float32) * fan_in ** (-0.5)
        return {'hidden_states': jax.random.normal(ks[0], (B, S, H), jnp.float32), 'router_w': w(ks[1], (E, H), H), 'w_gate': w(ks[2], (E, H, I_MOE), H), 'w_up': w(ks[3], (E, H, I_MOE), H), 'w_down': w(ks[4], (E, I_MOE, H), I_MOE), 'sh_gate': w(ks[5], (H, I_SH), H), 'sh_up': w(ks[6], (H, I_SH), H), 'sh_down': w(ks[7], (I_SH, H), I_SH), 'sh_gate_w': w(ks[8], (H, 1), H)}
    _L0_ffn_all = _L0_ffn_setup()
    _L0_ffn_in = {k: v for k, v in _L0_ffn_all.items() if k in ('router_w', 'w_gate', 'w_up', 'w_down', 'sh_gate', 'sh_up', 'sh_down', 'sh_gate_w')}
    del _L0_ffn_all
    return {'x': x, 'cond_2048': cond_2048, 'L0_cond_ada_w': _L0_cond_in['ada_w'], 'L0_cond_ada_b': _L0_cond_in['ada_b'], 'L0_cond_qkv_w': _L0_cond_in['qkv_w'], 'L0_cond_qkv_b': _L0_cond_in['qkv_b'], 'L0_cond_out_w': _L0_cond_in['out_w'], 'L0_cond_out_b': _L0_cond_in['out_b'], 'L0_cond_ffn_w1': _L0_cond_in['ffn_w1'], 'L0_cond_ffn_b1': _L0_cond_in['ffn_b1'], 'L0_cond_ffn_w2': _L0_cond_in['ffn_w2'], 'L0_cond_ffn_b2': _L0_cond_in['ffn_b2'], 'L0_ffn_router_w': _L0_ffn_in['router_w'], 'L0_ffn_w_gate': _L0_ffn_in['w_gate'], 'L0_ffn_w_up': _L0_ffn_in['w_up'], 'L0_ffn_w_down': _L0_ffn_in['w_down'], 'L0_ffn_sh_gate': _L0_ffn_in['sh_gate'], 'L0_ffn_sh_up': _L0_ffn_in['sh_up'], 'L0_ffn_sh_down': _L0_ffn_in['sh_down'], 'L0_ffn_sh_gate_w': _L0_ffn_in['sh_gate_w']}

def reference(x, cond_2048, L0_cond_ada_w, L0_cond_ada_b, L0_cond_qkv_w, L0_cond_qkv_b, L0_cond_out_w, L0_cond_out_b, L0_cond_ffn_w1, L0_cond_ffn_b1, L0_cond_ffn_w2, L0_cond_ffn_b2, L0_ffn_router_w, L0_ffn_w_gate, L0_ffn_w_up, L0_ffn_w_down, L0_ffn_sh_gate, L0_ffn_sh_up, L0_ffn_sh_down, L0_ffn_sh_gate_w):
    import jax
    import jax.numpy as jnp

    def _L0_cond_ref(x, timestep_embed, ada_w, ada_b, qkv_w, qkv_b, out_w, out_b, ffn_w1, ffn_b1, ffn_w2, ffn_b2):
        import jax, jax.numpy as jnp
        import numpy as np
        DIM = 256
        H = 16
        DH = 128
        INNER = H * DH
        MLP = 4 * DIM
        B, T = (2, 256)
        EPS = 1e-06

        def _ln(x):
            mu = jnp.mean(x, axis=-1, keepdims=True)
            var = jnp.var(x, axis=-1, keepdims=True)
            return (x - mu) * jax.lax.rsqrt(var + EPS)
        Bc, Tc, D = x.shape
        ada = (timestep_embed @ ada_w + ada_b)[:, None, :]
        shift1, scale1, gate1, shift2, scale2, gate2 = jnp.split(ada, 6, axis=-1)
        x1 = _ln(x) * (1.0 + scale1) + shift1
        qkv = (x1 @ qkv_w + qkv_b).reshape(Bc, Tc, 3, H, DH)
        q, k, v = (qkv[:, :, 0], qkv[:, :, 1], qkv[:, :, 2])
        scale = DH ** (-0.5)
        attn = jnp.einsum('bthd,bshd->bhts', q, k) * scale
        attn = jax.nn.softmax(attn, axis=-1)
        attn_out = jnp.einsum('bhts,bshd->bthd', attn, v).reshape(Bc, Tc, INNER)
        attn_out = attn_out @ out_w + out_b
        x = x + gate1 * attn_out
        x2 = _ln(x) * (1.0 + scale2) + shift2
        h = jax.nn.gelu(x2 @ ffn_w1 + ffn_b1, approximate=False)
        x = x + gate2 * (h @ ffn_w2 + ffn_b2)
        return x

    def _L0_ffn_ref(hidden_states, router_w, w_gate, w_up, w_down, sh_gate, sh_up, sh_down, sh_gate_w):
        import jax, jax.numpy as jnp
        import numpy as np
        B, S, H = (2, 256, 256)
        E, K = (16, 4)
        I_MOE, I_SH = (176, 704)
        orig = hidden_states.shape
        h = hidden_states.reshape(-1, orig[-1])
        N = h.shape[0]
        logits = h @ router_w.T
        probs = jax.nn.softmax(logits.astype(jnp.float32), axis=-1)
        top_vals, top_idx = jax.lax.top_k(probs, K)
        top_vals = top_vals / jnp.maximum(top_vals.sum(-1, keepdims=True), 1e-09)
        top_vals = top_vals.astype(h.dtype)
        comb = jnp.zeros((N, E), h.dtype).at[jnp.arange(N)[:, None], top_idx].add(top_vals)
        g = jnp.einsum('nh,ehi->eni', h, w_gate)
        u = jnp.einsum('nh,ehi->eni', h, w_up)
        y = jnp.einsum('eni,eih->enh', jax.nn.silu(g) * u, w_down)
        routed = jnp.einsum('enh,ne->nh', y, comb)
        shared = jax.nn.silu(h @ sh_gate) * (h @ sh_up) @ sh_down
        sg = jax.nn.sigmoid(h @ sh_gate_w)
        return (routed + sg * shared).reshape(orig)
    x = x + _L0_ffn_ref(_L0_cond_ref(x, cond_2048, L0_cond_ada_w, L0_cond_ada_b, L0_cond_qkv_w, L0_cond_qkv_b, L0_cond_out_w, L0_cond_out_b, L0_cond_ffn_w1, L0_cond_ffn_b1, L0_cond_ffn_w2, L0_cond_ffn_b2), L0_ffn_router_w, L0_ffn_w_gate, L0_ffn_w_up, L0_ffn_w_down, L0_ffn_sh_gate, L0_ffn_sh_up, L0_ffn_sh_down, L0_ffn_sh_gate_w)
    return x

_drawn_inputs = setup_inputs


def setup_inputs(seed=0):
    import zlib

    import numpy as np

    out = dict(_drawn_inputs(seed))
    spreads = {'L0_cond_ada_b': (0.0, 0.1),
     'L0_cond_qkv_b': (0.0, 0.1),
     'L0_cond_out_b': (0.0, 0.1),
     'L0_cond_ffn_b1': (0.0, 0.346),
     'L0_cond_ffn_b2': (0.0, 0.1)}
    factors = {}
    for name, (base, spread) in spreads.items():
        noise = np.random.default_rng([zlib.crc32(name.encode()), seed]).standard_normal(out[name].shape)
        drawn = base * np.exp(spread * noise) if base else spread * noise
        out[name] = jnp.asarray(drawn.astype(out[name].dtype))
    for name, factor in factors.items():
        out[name] = (out[name] * factor).astype(out[name].dtype)
    return out
```

```python
import concourse.bass as bass
from concourse import mybir
from contextlib import ExitStack

B, T, D = 16, 128, 256
H, DH = 16, 128
MLP = 1024
E, TOPK, I_MOE, I_SH = 16, 4, 176, 704
P = 128
KD = D // P
N = 512
TG = B * T // N
BG = N // T
HG = 2
NHG = H // HG
UNITS = NHG * TG
BODY = 2 * TG
SCALE = DH ** -0.5
LN_EPS = 1e-6
F1 = MLP // P
HID = E * I_MOE + I_SH
CH = -(-HID // P)
CG = 4
NCG = CH // CG
EG = E + 1
SELK = 32 + EG
LAG = 2


def adaln_moe_kernel(nc, x, condT, ada_w, bias, bqk, bv, wqkv, wo, w1, w2, router, wgu, wd, sel, ident, out):
    f32 = mybir.dt.float32
    f32r = mybir.dt.float32r
    ALU = mybir.AluOpType
    ACT = mybir.ActivationFunctionType
    AX = mybir.AxisListType

    ADA_B, OUT_B, B1, B2 = 0, 12, 14, 22
    SHIFT1, SCALE1, GATE1, SHIFT2, SCALE2, GATE2 = 0, 2, 4, 6, 8, 10

    x_tok_view = x.rearrange("(g b t) d -> g t b d", b=BG, t=T)
    out_view = out.rearrange("(g b t) d -> g t b d", b=BG, t=T)

    with ExitStack() as ctx:
        def sb(name, shape, dt=f32):
            return ctx.enter_context(nc.sbuf_tensor(name, shape, dt))

        def sem(name):
            return ctx.enter_context(nc.semaphore(name))

        arena_a = sb("arena_a", [P, 10240], f32r)
        arena_b = sb("arena_b", [P, 8192], f32r)
        tok_hl = sb("tok_hl", [P, 2, KD, B * T], f32r)
        x2_hl = sb("x2_hl", [P, 2, KD, N], f32r)
        hid_hl = sb("hid_hl", [P, 4, 2, N], f32r)
        wqkv_hl = arena_a[:, 0:6144].rearrange("p (r s k n) -> p r s k n", r=2, s=2, k=KD)
        wo_hl = arena_a[:, 6144:8192].rearrange("p (r s h n) -> p r s h n", r=2, s=2, h=HG)
        o_hl = arena_a[:, 8192:10240].rearrange("p (s h n) -> p s h n", s=2, h=HG)
        w1_hl = arena_b[:, 0:4096].rearrange("p (s k n) -> p s k n", s=2, k=KD)
        w2_hl = arena_b[:, 4096:8192].rearrange("p (s k n) -> p s k n", s=2, k=F1)
        wgu_hl = [a[:, 0:4096].rearrange("p (s k c g n) -> p s k c g n", s=2, k=KD, c=CG, g=2) for a in (arena_a, arena_b)]
        wd_hl = [a[:, 4096:6144].rearrange("p (s c n) -> p s c n", s=2, c=CG) for a in (arena_a, arena_b)]
        sel_r = [arena_a[0:SELK, o:o + CG * P].rearrange("p (c n) -> p c n", c=CG) for o in (6144, 6144 + CG * P)]
        comb_r = arena_b[:, 6144:8192]

        acc = sb("acc", [P, KD, B * T])
        raw = sb("raw", [P, 4096])
        bv_sb = sb("bv_sb", [P, 2, HG * DH])
        bqk_sb = sb("bqk_sb", [P, 2, 2 * HG])
        work = sb("work", [P, 8192])
        ada_sb = sb("ada_sb", [P, 12, B])
        bias_sb = sb("bias_sb", [P, 24])
        cond_sb = sb("cond_sb", [P, KD, B])
        router_sb = sb("router_sb", [P, KD, EG])
        id_sb = sb("id_sb", [P, P])
        stats = sb("stats", [P, BG, 6])
        mv = sb("mv", [P, 2, BG, 2])
        veps = sb("veps", [P, 2, BG])
        rstd = sb("rstd", [P, 2, BG])
        mhalf = sb("mhalf", [P, BG])
        ones = sb("ones", [P, 1])
        rmax = sb("rmax", [P, 2, BG])
        negm = sb("negm", [P, 2, BG])
        rsum = sb("rsum", [P, 2, BG])
        rinv = sb("rinv", [P, 2, BG])

        ada_w_sb = acc[:, :, 0:1536]
        x_in = work[:, 0:2048].rearrange("p (r b d) -> p r b d", r=2, b=BG)
        xhat1 = work[:, 2048:4096].rearrange("p (r b d) -> p r b d", r=2, b=BG)
        mod1 = work[:, 4096:6144].rearrange("p (r k n) -> p r k n", r=2, k=KD)
        raw_qkv = [raw[:, r * 2048:r * 2048 + 1536].rearrange("p (k n) -> p k n", k=KD) for r in range(2)]
        raw_o = [raw[:, r * 2048 + 1536:r * 2048 + 2048].rearrange("p (h n) -> p h n", h=HG) for r in range(2)]
        qT = work[:, 0:2048].rearrange("p (r h n) -> p r h n", r=2, h=HG)
        kT = work[:, 2048:4096].rearrange("p (r h n) -> p r h n", r=2, h=HG)
        v_sb = work[:, 4096:6144].rearrange("p (r b n) -> p r b n", r=2, b=BG)
        probs = work[:, 6144:7168].rearrange("p (r j n) -> p r j n", r=2, j=4)
        probsT = work[:, 7168:8192].rearrange("p (r j n) -> p r j n", r=2, j=4)
        raw_w1 = raw[:, 0:2048].rearrange("p (k n) -> p k n", k=KD)
        raw_w2 = raw[:, 2048:4096].rearrange("p (k n) -> p k n", k=F1)
        raw_gu = raw[:, 0:2048]
        raw_d = raw[:, 2048:3072]
        raw_sel = raw[0:SELK, 3072:3072 + CG * P]
        x_tok2 = work[:, 0:1024].rearrange("p (b d) -> p b d", b=BG)
        yT = work[:, 1024:2048].rearrange("p (k n) -> p k n", k=KD)
        hT = work[:, 2048:3072].rearrange("p (k n) -> p k n", k=KD)
        xhat2 = work[:, 3072:4096].rearrange("p (b d) -> p b d", b=BG)
        part = work[:, 4096:5120].rearrange("p (k n) -> p k n", k=KD)
        gel = work[:, 5120:6144].rearrange("p (r n) -> p r n", r=2)
        def rt(i, n):
            return work[:, 4096 + 512 * i:4096 + 512 * i + B * n].rearrange("p (b e) -> p b e", b=B)
        logits = sb("logits", [P, B, EG])
        shifted, expd, pr, top, rest, comb = rt(0, E), rt(1, EG), rt(2, E), rt(3, 8), rt(4, E), rt(5, EG)
        r_small = work[:, 4096 + 512 * 6:8192].rearrange("p (i b) -> p i b", b=B)
        sil = work[:, 0:1024].rearrange("p (r n) -> p r n", r=2)
        gu = work[:, 1024:2048].rearrange("p (r n) -> p r n", r=2)
        hw = work[:, 2048:3072].rearrange("p (r n) -> p r n", r=2)
        x_fin = work[:, 4096:6144].rearrange("p (r b d) -> p r b d", r=2, b=BG)
        y_fin = work[:, 6144:8192].rearrange("p (r b d) -> p r b d", r=2, b=BG)

        bank = [ctx.enter_context(nc.psum_tensor(f"bank{i}", [P, N], f32)) for i in range(8)]
        PROJ, SC, PT, OB, OP = bank[0:2], bank[2:4], bank[4], bank[5], bank[6:8]
        GATE, UP, COMB, DOWN = bank[0:2], bank[2:4], bank[4:6], bank[6:8]

        s_load = sem("s_load")
        s_x = [sem("s_x0"), sem("s_x1")]
        s_raw = [sem("s_raw0"), sem("s_raw1")]
        s_w1raw, s_w2raw = sem("s_w1raw"), sem("s_w2raw")
        s_graw = sem("s_graw")
        s_pool = sem("s_pool")
        s_act = sem("s_act")
        s_v = sem("s_v")
        s_ada_mm = sem("s_ada_mm")
        s_ada = sem("s_ada")
        s_var = sem("s_var")
        s_rstd = sem("s_rstd")
        s_xhat = sem("s_xhat")
        s_xT = sem("s_xT")
        s_mod = sem("s_mod")
        s_x1h = sem("s_x1h")
        s_x1l = sem("s_x1l")
        s_wq = sem("s_wq")
        s_wo = sem("s_wo")
        s_pj = sem("s_pj")
        s_qk = sem("s_qk")
        s_vv = sem("s_vv")
        s_s = sem("s_s")
        s_negm = sem("s_negm")
        s_exp = sem("s_exp")
        s_pn = sem("s_pn")
        s_t = sem("s_t")
        s_pt = sem("s_pt")
        s_av = sem("s_av")
        s_oh = sem("s_oh")
        s_ol = sem("s_ol")
        s_op = sem("s_op")
        s_acc = sem("s_acc")
        s_clr = sem("s_clr")
        s_w12 = sem("s_w12")
        s_xt2 = sem("s_xt2")
        s_x2in = sem("s_x2in")
        s_y = sem("s_y")
        s_yt = sem("s_yt")
        s_f1 = sem("s_f1")
        s_gel = sem("s_gel")
        s_fh = sem("s_fh")
        s_fl = sem("s_fl")
        s_f2 = sem("s_f2")
        s_h = sem("s_h")
        s_hh = sem("s_hh")
        s_rl = sem("s_rl")
        s_log = sem("s_log")
        s_re = sem("s_re")
        s_rx = sem("s_rx")
        s_comb = sem("s_comb")
        s_cT = sem("s_cT")
        s_ch = sem("s_ch")
        s_cl = sem("s_cl")
        s_wgu = sem("s_wgu")
        s_wdn = sem("s_wdn")
        s_wg = sem("s_wg")
        s_t1 = sem("s_t1")
        s_hl = sem("s_hl")
        s_czero = sem("s_czero")
        s_gu = sem("s_gu")
        s_g = sem("s_g")
        s_sil = sem("s_sil")
        s_hw = sem("s_hw")
        s_hh3 = sem("s_hh3")
        s_hl3 = sem("s_hl3")
        s_d = sem("s_d")
        s_da = sem("s_da")
        s_xf = [sem("s_xf0"), sem("s_xf1")]
        s_fT = sem("s_fT")
        s_fin = sem("s_fin")
        s_out = [sem("s_out0"), sem("s_out1")]

        PARTS = ((0, 0), (0, 1), (1, 0))

        block = ctx.enter_context(nc.Block())

        def flat(ap):
            dims = " ".join("abcd"[:len(ap.shape) - 1])
            return ap.rearrange(f"p {dims} -> p ({dims})")

        def split(eng, halves, whole, done, own, high=None):
            high = s_pool if high is None else high
            hi, lo, whole = flat(halves[:, 0]), flat(halves[:, 1]), flat(whole)
            eng.tensor_tensor(hi, whole, ones[:, 0:1].to_broadcast(whole.shape), ALU.mult).then_inc(high, 1)
            eng.wait_ge(high, own)
            eng.tensor_tensor(lo, whole, hi.bitcast(f32), ALU.subtract).then_inc(done, 1)

        @block.sync
        def _(sp):
            sp.dma_start(cond_sb[:, :, :], condT).then_inc(s_load, 16)
            sp.dma_start(ada_w_sb, ada_w).then_inc(s_load, 16)
            sp.dma_start(bias_sb[:, :], bias).then_inc(s_load, 16)
            sp.dma_start(id_sb[:, :], ident).then_inc(s_load, 16)
            sp.dma_start(router_sb[:, :, :], router).then_inc(s_load, 16)
            def load_heads(hg, r):
                sp.dma_start(raw_qkv[r], wqkv[hg]).then_inc(s_raw[r], 16)
                sp.dma_start(raw_o[r], wo[hg]).then_inc(s_raw[r], 16)
                sp.dma_start(bqk_sb[:, r], bqk[hg]).then_inc(s_raw[r], 16)
                sp.dma_start(bv_sb[:, r], bv[hg].to_broadcast([P, HG * DH])).then_inc(s_raw[r], 16)

            def load_group(g):
                sp.dma_start(raw_gu, wgu[g]).then_inc(s_graw, 16)
                sp.dma_start(raw_d, wd[g]).then_inc(s_graw, 16)
                sp.dma_start(raw_sel, sel[g]).then_inc(s_graw, 16)

            load_heads(0, 0)
            for g in range(TG):
                if g >= 2:
                    sp.wait_ge(s_xhat, g - 1)
                sp.dma_start(x_in[:, g % 2], x_tok_view[g]).then_inc(s_x[g % 2], 16)
            load_heads(1, 1)
            with sp.Fori(1, NHG // 2) as it:
                for r in range(2):
                    sp.wait_ge(s_wo, 2 * it + (r - 1))
                    sp.wait_ge(s_vv, 16 * it + (8 * r - 8))
                    load_heads(2 * it + r, r)
            sp.wait_ge(s_wo, NHG)
            sp.dma_start(raw_w1, w1).then_inc(s_w1raw, 16)
            sp.dma_start(raw_w2, w2).then_inc(s_w2raw, 16)
            sp.wait_ge(s_w12, 2)
            load_group(0)
            sp.wait_ge(s_op, 2 * UNITS)
            for g in range(TG):
                if g >= 1:
                    sp.wait_ge(s_xt2, g)
                sp.dma_start(x_tok2, x_tok_view[g]).then_inc(s_x2in, 16)
            with sp.Fori(1, NCG) as g:
                sp.wait_ge(s_wg, g)
                load_group(g)
            sp.wait_ge(s_ch, 1)
            for g in range(TG):
                if g >= 2:
                    sp.wait_ge(s_fin, g - 1)
                sp.dma_start(x_fin[:, g % 2], x_tok_view[g]).then_inc(s_xf[g % 2], 16)
                if g >= 1:
                    sp.wait_ge(s_fin, g)
                    sp.dma_start(out_view[g - 1], y_fin[:, (g - 1) % 2]).then_inc(s_out[(g - 1) % 2], 16)
            sp.wait_ge(s_fin, TG)
            sp.dma_start(out_view[TG - 1], y_fin[:, (TG - 1) % 2]).then_inc(s_out[(TG - 1) % 2], 16)
            sp.wait_ge(s_out[0], 16 * TG // 2)
            sp.wait_ge(s_out[1], 16 * TG // 2)

        def split_group(eng, r, own, done=None):
            split(eng, wgu_hl[r], raw_gu.rearrange("p (k c g n) -> p k c g n", k=KD, c=CG, g=2), s_wgu, own, done)
            split(eng, wd_hl[r], raw_d.rearrange("p (c n) -> p c n", c=CG), s_wdn, own + 1, done)
            eng.tensor_copy(sel_r[r], raw_sel.rearrange("p (c n) -> p c n", c=CG)).then_inc(s_wg, 1)

        @block.gpsimd
        def _(pool):
            pool.memset(mhalf[:, :], -0.5).then_inc(s_pool, 1)
            pool.memset(ones[:, :], 1.0).then_inc(s_pool, 1)
            own = 2

            def inverse_root(g, r, own):
                pool.wait_ge(s_var, g + 1)
                pool.tensor_scalar(veps[:, r], mv[:, r, :, 1], LN_EPS, None, ALU.add).then_inc(s_pool, 1)
                pool.wait_ge(s_pool, own + 1)
                pool.tensor_tensor(rstd[:, r], veps[:, r], mhalf[:, :], ALU.pow).then_inc(s_rstd, 1)
                return own + 1

            for g in range(TG):
                if g >= 2:
                    pool.wait_ge(s_xhat, g - 1)
                own = inverse_root(g, g % 2, own)
                if g == 0:
                    pool.wait_ge(s_raw[0], 64)
                    split(pool, wqkv_hl[:, 0], raw_qkv[0], s_wq, own + 1)
                    own += 1
            split(pool, wo_hl[:, 0], raw_o[0], s_wo, own + 1)
            pool.wait_ge(s_ada_mm, 1)
            pool.memset(acc[:, :, :], 0.0).then_inc(s_clr, 1)
            pool.wait_ge(s_raw[1], 64)
            split(pool, wqkv_hl[:, 1], raw_qkv[1], s_wq, own + 2)
            split(pool, wo_hl[:, 1], raw_o[1], s_wo, own + 3)
            own += 3
            with pool.Fori(1, NHG // 2) as it:
                for r in range(2):
                    pool.wait_ge(s_raw[r], 64 * it + 64)
                    pool.wait_ge(s_pj, 48 * it + (24 * r - 24))
                    split(pool, wqkv_hl[:, r], raw_qkv[r], s_wq, 4 * it + (own - 4 + 2 * r + 1))
                    pool.wait_ge(s_op, 16 * it + (8 * r - 8))
                    split(pool, wo_hl[:, r], raw_o[r], s_wo, 4 * it + (own - 4 + 2 * r + 2))
            own += 4 * (NHG // 2 - 1)
            pool.wait_ge(s_w1raw, 16)
            split(pool, w1_hl, raw_w1, s_w12, own + 1)
            pool.wait_ge(s_w2raw, 16)
            split(pool, w2_hl, raw_w2, s_w12, own + 2)
            own += 2
            for g in range(TG):
                own = inverse_root(TG + g, 0, own)
            pool.wait_ge(s_t1, KD * TG)
            pool.memset(acc[:, :, :], 0.0).then_inc(s_clr, 1)
            pool.wait_ge(s_graw, 96)
            pool.wait_ge(s_f2, TG)
            split_group(pool, 1, own + 1)
            own += 2
            with pool.Fori(1, NCG // 2) as it:
                for r in range(2):
                    pool.wait_ge(s_graw, 96 * it + (48 * r + 48))
                    pool.wait_ge(s_d, 8 * it + (4 * r - 4))
                    split_group(pool, r, 4 * it + (own - 4 + 2 * r + 1))
            own += 4 * (NCG // 2 - 1)
            pool.wait_ge(s_graw, 48 * NCG)
            pool.wait_ge(s_d, TG * (NCG - 2))
            split_group(pool, 0, own + 1)

        def n_of(it, j, per, c):
            return per * BODY * it + (per * j + c)

        @block.scalar
        def _(act):
            for g in range(TG):
                for c in range(KD):
                    act.wait_ge(s_mod, KD * g + c + 1)
                    nc.scalar.activation(tok_hl[:, 0, c, N * g:N * g + N], mod1[:, g % 2, c], ACT.Copy)\
                        .then_inc(s_x1h, 1)

            def project(it, j, tile):
                act.wait_ge(s_pj, n_of(it, j, 6, tile + 1))
                dst = (qT if tile < HG else kT)[:, j % 2, tile % HG]
                r = (j % BODY) // TG
                nc.scalar.activation(dst, PROJ[tile % 2][:, :], ACT.Identity,
                                     bias=bqk_sb[:, r, tile:tile + 1]).then_inc(s_qk, 1)

            def attend(it, j, more):
                for m in range(2):
                    act.wait_ge(s_negm, n_of(it, j, 2, m + 1))
                    for i in range(4):
                        last = nc.scalar.activation(probs[:, m, i], SC[m][:, i * T:i * T + T], ACT.Exp,
                                                    bias=negm[:, m, i:i + 1], scale=SCALE,
                                                    accum_out=rsum[:, m, i:i + 1])
                    last.then_inc(s_exp, 1)
                    if more:
                        project(it, j + 1, m)
                for m in range(2):
                    act.wait_ge(s_t, n_of(it, j, 2, m + 1))
                    nc.scalar.activation(probsT[:, m], PT[:, :].rearrange("p (i n) -> p i n", i=4), ACT.Copy)\
                        .then_inc(s_pt, 1)
                    if more:
                        project(it, j + 1, 2 + m)
                    act.wait_ge(s_av, n_of(it, j, 2, m + 1))
                    nc.scalar.activation(o_hl[:, 0, :, 256 * m:256 * m + 256],
                                         OB[:, :].rearrange("p (h n) -> p h n", h=HG), ACT.Copy).then_inc(s_oh, 1)

            act.wait_ge(s_raw[0], 64)
            for tile in range(4):
                project(0, 0, tile)
            with act.Fori(0, NHG // 2 - 1) as it:
                for j in range(BODY):
                    if j == TG - 1:
                        act.wait_ge(s_raw[1], 64 * it + 64)
                    if j == BODY - 1:
                        act.wait_ge(s_raw[0], 64 * it + 128)
                    attend(it, j, True)
            for j in range(BODY):
                if j == TG - 1:
                    act.wait_ge(s_raw[1], 64 * NHG // 2)
                attend(NHG // 2 - 1, j, j < BODY - 1)

            for g in range(TG):
                for c in range(KD):
                    act.wait_ge(s_mod, KD * (TG + g) + c + 1)
                    nc.scalar.activation(x2_hl[:, 0, c], part[:, c], ACT.Copy).then_inc(s_x1h, 1)
                for c in range(F1):
                    k = F1 * g + c
                    act.wait_ge(s_f1, k + 1)
                    if k >= 2:
                        act.wait_ge(s_fl, k - 1)
                    nc.scalar.activation(gel[:, c % 2], bank[c % 2][:, :], ACT.Gelu,
                                         bias=bias_sb[:, B1 + c:B1 + c + 1]).then_inc(s_gel, 1)
                    act.wait_ge(s_gel, k + 1)
                    nc.scalar.activation(hid_hl[:, c % 4, 0], gel[:, c % 2], ACT.Copy).then_inc(s_fh, 1)
                for c in range(KD):
                    act.wait_ge(s_h, KD * g + c + 1)
                    nc.scalar.activation(tok_hl[:, 0, c, N * g:N * g + N], hT[:, c], ACT.Copy).then_inc(s_hh, 1)
            act.wait_ge(s_re, 1)
            nc.scalar.activation(expd[:, :, 0:E], shifted, ACT.Exp)
            nc.scalar.activation(expd[:, :, E:EG], logits[:, :, E:EG], ACT.Exp, scale=-1.0).then_inc(s_rx, 1)

            def chunk(k0, i):
                act.wait_ge(s_g, k0 + (i + 1))
                nc.scalar.activation(sil[:, i % 2], GATE[i % 2][:, :], ACT.Silu).then_inc(s_sil, 1)
                act.wait_ge(s_hw, k0 + (i + 1))
                nc.scalar.activation(hid_hl[:, i % 4, 0], hw[:, i % 2], ACT.Copy).then_inc(s_hh3, 1)

            act.wait_ge(s_czero, 1)
            for g in range(TG):
                act.wait_ge(s_cT, g + 1)
                nc.scalar.activation(comb_r[0:EG, N * g:N * g + N], bank[4 + g % 2][0:EG, :], ACT.Copy)\
                    .then_inc(s_ch, 1)
            with act.Fori(0, NCG // 2) as it:
                for i in range(2 * TG * CG):
                    chunk(2 * TG * CG * it, i)
            for i in range(TG * CG):
                chunk(2 * TG * CG * (NCG // 2), i)

        @block.vector
        def _(dve):
            own = 0

            dve.wait_ge(s_ada_mm, 1)
            dve.wait_ge(s_load, 80)
            nc.vector.tensor_tensor(ada_sb[:, :, :], bank[0][:, 0:12 * B].rearrange("p (c b) -> p c b", b=B),
                                    bias_sb[:, ADA_B:ADA_B + 12].unsqueeze(2).to_broadcast([P, 12, B]),
                                    ALU.add).then_inc(s_v, 1)
            dve.wait_ge(s_v, 1)
            for c in (SCALE1, SCALE2):
                nc.vector.tensor_scalar(ada_sb[:, c:c + KD], ada_sb[:, c:c + KD], 1.0, None, ALU.add)\
                    .then_inc(s_v, 1)
            own = 3
            dve.wait_ge(s_v, own)

            def ada_of(c, g):
                return ada_sb[:, c, BG * g:BG * g + BG].unsqueeze(2).to_broadcast([P, BG, T])

            def by_batch(ap):
                return ap.rearrange("p (b t) -> p b t", b=BG)

            def statistics(source, r, own):
                for b in range(BG):
                    nc.vector.bn_stats(out=stats[:, b], in_=source(b)).then_inc(s_v, 1)
                dve.wait_ge(s_v, own + BG)
                for b in range(BG):
                    last = nc.vector.bn_aggr(out=mv[:, r, b], in_=stats[:, b])
                last.then_inc(s_var, 1)
                return own + BG

            def normalise(g, source, target, r):
                dve.wait_ge(s_rstd, g + 1)
                for b in range(BG):
                    last = nc.vector.tensor_scalar(target[:, b], source(b), mv[:, r, b, 0:1], rstd[:, r, b:b + 1],
                                                   ALU.subtract, ALU.mult)
                last.then_inc(s_xhat, 1)

            def modulate(g, turned, target, scale, shift, own):
                for c in range(KD):
                    nc.vector.tensor_tensor(by_batch(target[:, c]), by_batch(turned[c][:, :]), ada_of(scale + c, g),
                                            ALU.mult).then_inc(s_v, 1)
                    dve.wait_ge(s_v, own + 1)
                    nc.vector.tensor_tensor(by_batch(target[:, c]), by_batch(target[:, c]), ada_of(shift + c, g),
                                            ALU.add).then_inc(s_mod, 1)
                    own += 1
                return own

            def low_half(target, whole, high):
                return nc.vector.tensor_tensor(target, whole, high.bitcast(f32), ALU.subtract)

            def first_part(g, own):
                dve.wait_ge(s_x[g % 2], 16 * (g // 2 + 1))
                own = statistics(lambda b: x_in[:, g % 2, b], g % 2, own)
                normalise(g, lambda b: x_in[:, g % 2, b], xhat1[:, g % 2], g % 2)
                return own

            def second_part(g, own):
                dve.wait_ge(s_xT, g + 1)
                own = modulate(g, bank[2 + 2 * (g % 2):4 + 2 * (g % 2)], mod1[:, g % 2], SCALE1, SHIFT1, own)
                for c in range(KD):
                    dve.wait_ge(s_x1h, KD * g + c + 1)
                    low_half(tok_hl[:, 1, c, N * g:N * g + N], mod1[:, g % 2, c], tok_hl[:, 0, c, N * g:N * g + N])\
                        .then_inc(s_x1l, 1)
                return own

            own = first_part(0, own)
            for g in range(TG):
                if g + 1 < TG:
                    own = first_part(g + 1, own)
                own = second_part(g, own)

            def head(it, j, base):
                for m in range(2):
                    dve.wait_ge(s_s, n_of(it, j, 2, m + 1))
                    nc.vector.tensor_reduce(rmax[:, m], SC[m][:, :].rearrange("p (i n) -> p i n", i=4), AX.X, ALU.max)\
                        .then_inc(s_v, 1)
                    dve.wait_ge(s_v, n_of(it, j, 4, base + m + 1))
                    nc.vector.tensor_scalar(negm[:, m], rmax[:, m], -SCALE, None, ALU.mult).then_inc(s_negm, 1)
                normal(it, j, base, 0)

            def normal(it, j, base, m):
                dve.wait_ge(s_exp, n_of(it, j, 2, m + 1))
                nc.vector.reciprocal(rinv[:, m], rsum[:, m]).then_inc(s_v, 1)
                dve.wait_ge(s_v, n_of(it, j, 4, base + 3 + m))
                nc.vector.tensor_tensor(probs[:, m], probs[:, m], rinv[:, m].unsqueeze(2).to_broadcast([P, 4, T]),
                                        ALU.mult).then_inc(s_pn, 1)

            def add_projection(it, j):
                g = j % TG
                for m in range(KD):
                    dve.wait_ge(s_op, n_of(it, j, 2, m + 1))
                    here = acc[:, m, N * g:N * g + N]
                    nc.vector.tensor_tensor(here, OP[m][:, :], here, ALU.add).then_inc(s_acc, 1)

            def project_v(it, j, tile):
                dve.wait_ge(s_pj, n_of(it, j, 6, 4 + tile + 1))
                r = (j % BODY) // TG
                nc.vector.tensor_tensor(v_sb[:, j % 2, 2 * tile:2 * tile + 2],
                                        PROJ[tile][:, :].rearrange("p (b n) -> p b n", b=2),
                                        bv_sb[:, r].unsqueeze(1).to_broadcast([P, 2, HG * DH]), ALU.add)\
                    .then_inc(s_vv, 1)

            def tail(it, j, base, more):
                normal(it, j, base, 1)
                for m in range(2):
                    dve.wait_ge(s_oh, n_of(it, j, 2, m + 1))
                    low_half(o_hl[:, 1, :, 256 * m:256 * m + 256], OB[:, :].rearrange("p (h n) -> p h n", h=HG),
                             o_hl[:, 0, :, 256 * m:256 * m + 256]).then_inc(s_ol, 1)
                    if more:
                        project_v(it, j + 1, m)

            dve.wait_ge(s_raw[0], 64)
            for tile in range(2):
                project_v(0, 0, tile)
            dve.wait_ge(s_clr, 1)
            base = own
            head(0, 0, base)
            with dve.Fori(0, NHG // 2 - 1) as it:
                for j in range(BODY):
                    if j == TG - 1:
                        dve.wait_ge(s_raw[1], 64 * it + 64)
                    if j == BODY - 1:
                        dve.wait_ge(s_raw[0], 64 * it + 128)
                    tail(it, j, base, True)
                    head(it, j + 1, base)
                    add_projection(it, j)
            for j in range(BODY):
                it = NHG // 2 - 1
                if j == TG - 1:
                    dve.wait_ge(s_raw[1], 64 * NHG // 2)
                tail(it, j, base, j < BODY - 1)
                if j < BODY - 1:
                    head(it, j + 1, base)
                add_projection(it, j)
            own += 4 * UNITS

            dve.wait_ge(s_acc, KD * UNITS)
            for g in range(TG):
                cols = slice(N * g, N * g + N)
                for c in range(KD):
                    nc.vector.scalar_tensor_tensor(out=by_batch(yT[:, c]), in0=by_batch(acc[:, c, cols]),
                                                   scalar=bias_sb[:, OUT_B + c:OUT_B + c + 1], in1=ada_of(GATE1 + c, g),
                                                   op0=ALU.add, op1=ALU.mult).then_inc(s_t1, 1)
                    dve.wait_ge(s_t1, KD * g + c + 1)
                    dve.wait_ge(s_xt2, g + 1)
                    nc.vector.tensor_tensor(yT[:, c], bank[2 + c][:, :], yT[:, c], ALU.add).then_inc(s_y, 1)
                dve.wait_ge(s_yt, g + 1)

                def source(b):
                    return bank[4 + b // 2][:, D * (b % 2):D * (b % 2) + D]
                own = statistics(source, 0, own)
                normalise(TG + g, source, xhat2, 0)
                dve.wait_ge(s_xT, TG + g + 1)
                own = modulate(g, bank[2:4], part, SCALE2, SHIFT2, own)
                for c in range(KD):
                    dve.wait_ge(s_x1h, KD * (TG + g) + c + 1)
                    low_half(x2_hl[:, 1, c], part[:, c], x2_hl[:, 0, c]).then_inc(s_x1l, 1)
                for c in range(F1):
                    dve.wait_ge(s_fh, F1 * g + c + 1)
                    low_half(hid_hl[:, c % 4, 1], gel[:, c % 2], hid_hl[:, c % 4, 0]).then_inc(s_fl, 1)
                    if g == 0 and c == 0:
                        dve.wait_ge(s_graw, 48)
                        split_group(nc.vector, 0, own + 1, done=s_v)
                        own += 2
                dve.wait_ge(s_f2, g + 1)
                for c in range(KD):
                    nc.vector.scalar_tensor_tensor(out=by_batch(part[:, c]), in0=by_batch(bank[6 + c][:, :]),
                                                   scalar=bias_sb[:, B2 + c:B2 + c + 1], in1=ada_of(GATE2 + c, g),
                                                   op0=ALU.add, op1=ALU.mult).then_inc(s_v, 1)
                    own += 1
                    dve.wait_ge(s_v, own)
                    if g >= 1:
                        dve.wait_ge(s_rl, g)
                    nc.vector.tensor_tensor(hT[:, c], part[:, c], yT[:, c], ALU.add).then_inc(s_h, 1)
                for c in range(KD):
                    dve.wait_ge(s_hh, KD * g + c + 1)
                    low_half(tok_hl[:, 1, c, cols], hT[:, c], tok_hl[:, 0, c, cols]).then_inc(s_hl, 1)
                dve.wait_ge(s_rl, g + 1)
                nc.vector.tensor_copy(logits[:, BG * g:BG * g + BG],
                                      bank[4][:, 0:BG * EG].rearrange("p (b e) -> p b e", b=BG)).then_inc(s_log, 1)

            def step(ins, own):
                ins.then_inc(s_v, 1)
                dve.wait_ge(s_v, own + 1)
                return own + 1

            def small(i):
                return r_small[:, i]

            def along(ap, n):
                return ap.unsqueeze(2).to_broadcast([P, B, n])

            dve.wait_ge(s_log, TG)
            own = step(nc.vector.tensor_reduce(small(0), logits[:, :, 0:E], AX.X, ALU.max), own)
            nc.vector.tensor_tensor(shifted, logits[:, :, 0:E], along(small(0), E), ALU.subtract).then_inc(s_re, 1)
            dve.wait_ge(s_rx, 1)
            own = step(nc.vector.tensor_reduce(small(1), expd[:, :, 0:E], AX.X, ALU.add), own)
            own = step(nc.vector.reciprocal(small(2), small(1)), own)
            own = step(nc.vector.tensor_tensor(pr, expd[:, :, 0:E], along(small(2), E), ALU.mult), own)
            for b in range(B):
                last = nc.vector.max(out=top[:, b], in_=pr[:, b])
            own = step(last, own)
            own = step(nc.vector.tensor_reduce(small(3), top[:, :, 0:TOPK], AX.X, ALU.add), own)
            own = step(nc.vector.memset(top[:, :, TOPK:8], -1.0), own)
            for b in range(B):
                last = nc.vector.match_replace(out=rest[:, b], in_to_replace=top[:, b], in_values=pr[:, b],
                                               imm_value=0.0)
            own = step(last, own)
            own = step(nc.vector.tensor_scalar(small(4), small(3), 1e-9, None, ALU.max), own)
            own = step(nc.vector.reciprocal(small(5), small(4)), own)
            own = step(nc.vector.tensor_tensor(pr, pr, rest, ALU.subtract), own)
            nc.vector.tensor_tensor(comb[:, :, 0:E], pr, along(small(5), E), ALU.mult)
            own = step(nc.vector.tensor_scalar(small(6), expd[:, :, E], 1.0, None, ALU.add), own)
            nc.vector.reciprocal(comb[:, :, E], small(6)).then_inc(s_comb, 1)

            dve.wait_ge(s_f2, TG)
            nc.vector.memset(comb_r.bitcast(f32), 0.0).then_inc(s_czero, 1)
            for g in range(TG):
                dve.wait_ge(s_ch, g + 1)
                low_half(comb_r[32:32 + EG, N * g:N * g + N], bank[4 + g % 2][0:EG, :],
                         comb_r[0:EG, N * g:N * g + N]).then_inc(s_cl, 1)

            def chunk(k0, i):
                dve.wait_ge(s_sil, k0 + (i + 1))
                nc.vector.tensor_tensor(gu[:, i % 2], UP[i % 2][:, :], sil[:, i % 2], ALU.mult).then_inc(s_gu, 1)
                dve.wait_ge(s_gu, k0 + (i + 1))
                nc.vector.tensor_tensor(hw[:, i % 2], COMB[i % 2][:, :], gu[:, i % 2], ALU.mult).then_inc(s_hw, 1)
                dve.wait_ge(s_hh3, k0 + (i + 1))
                low_half(hid_hl[:, i % 4, 1], hw[:, i % 2], hid_hl[:, i % 4, 0]).then_inc(s_hl3, 1)

            def add_down(u0, u):
                dve.wait_ge(s_d, u0 + (u + 1))
                for c in range(KD):
                    here = acc[:, c, N * (u % TG):N * (u % TG) + N]
                    nc.vector.tensor_tensor(here, DOWN[c][:, :], here, ALU.add).then_inc(s_da, 1)

            dve.wait_ge(s_clr, 2)
            dve.sem_inc(s_da, 1)
            chunk(0, 0)
            with dve.Fori(0, NCG // 2) as it:
                for i in range(2 * TG * CG):
                    chunk(2 * TG * CG * it, i + 1)
                    if i % CG == CG - 1:
                        add_down(2 * TG * it, i // CG)
            k0, u0 = 2 * TG * CG * (NCG // 2), 2 * TG * (NCG // 2)
            for i in range(TG * CG):
                if i + 1 < TG * CG:
                    chunk(k0, i + 1)
                if i % CG == CG - 1:
                    add_down(u0, i // CG)

            for g in range(TG):
                dve.wait_ge(s_fT, g + 1)
                dve.wait_ge(s_xf[g % 2], 16 * (g // 2 + 1))
                if g >= 2:
                    dve.wait_ge(s_out[g % 2], 16)
                for m in range(2):
                    last = nc.vector.tensor_tensor(y_fin[:, g % 2, 2 * m:2 * m + 2],
                                                   bank[2 * (g % 2) + m][:, :].rearrange("p (b d) -> p b d", b=2),
                                                   x_fin[:, g % 2, 2 * m:2 * m + 2], ALU.add)
                last.then_inc(s_fin, 1)

        @block.tensor
        def _(pe):
            def exact(out_ap, stationary, moving, start, stop):
                for i, (s, m) in enumerate(PARTS):
                    last = nc.tensor.matmul(out_ap, stationary(s), moving(m), start=start and i == 0,
                                            stop=stop and i == len(PARTS) - 1)
                return last

            pe.wait_ge(s_load, 80)
            for c in range(12):
                for k in range(KD):
                    last = nc.tensor.matmul(bank[0][:, B * c:B * c + B], ada_w_sb[:, k, P * c:P * c + P], cond_sb[:, k],
                                            start=k == 0, stop=k == KD - 1)
            last.then_inc(s_ada_mm, 1)

            def turn_tokens(source, target):
                for c in range(KD):
                    for b in range(BG):
                        last = nc.tensor.transpose(target[c][:, T * b:T * b + T], source(b, c), id_sb[:, :])
                return last

            for g in range(TG):
                pe.wait_ge(s_xhat, g + 1)
                if g >= 2:
                    pe.wait_ge(s_mod, KD * (g - 1))
                turn_tokens(lambda b, c: xhat1[:, g % 2, b, c * P:c * P + P],
                            bank[2 + 2 * (g % 2):4 + 2 * (g % 2)]).then_inc(s_xT, 1)

            def project(it, j, tile):
                g, r = j % TG, (j % BODY) // TG
                if g == 0 and tile == 0:
                    pe.wait_ge(s_wq, (BODY // TG) * it + (j // TG + 1))
                first = isinstance(it, int) and it == 0 and j == 0
                if tile < 2:
                    if not first:
                        pe.wait_ge(s_vv, n_of(it, j, 2, tile - 1))
                else:
                    pe.wait_ge(s_qk, n_of(it, j, 4, tile - 1))
                if tile < 4:
                    for k in range(KD):
                        last = exact(PROJ[tile % 2][:, :],
                                     lambda s: wqkv_hl[:, r, s, k, tile * DH:tile * DH + DH],
                                     lambda s: tok_hl[:, s, k, N * g:N * g + N], k == 0, k == KD - 1)
                else:
                    for b in range(2):
                        col = N * g + T * (2 * (tile - 4) + b)
                        for k in range(KD):
                            last = exact(PROJ[tile % 2][:, HG * DH * b:HG * DH * (b + 1)],
                                         lambda s: tok_hl[:, s, k, col:col + T],
                                         lambda s: wqkv_hl[:, r, s, k, 2 * HG * DH:3 * HG * DH], k == 0, k == KD - 1)
                last.then_inc(s_pj, 1)

            def scores(it, j, m):
                if m == 0:
                    pe.wait_ge(s_qk, n_of(it, j, 4, 4))
                if not (isinstance(it, int) and it == 0 and j == 0):
                    pe.wait_ge(s_exp, n_of(it, j, 2, m - 1))
                for b in range(2):
                    for h in range(HG):
                        i, col = HG * b + h, T * (2 * m + b)
                        last = nc.tensor.matmul(SC[m][:, i * T:i * T + T], qT[:, j % 2, h, col:col + T],
                                                kT[:, j % 2, h, col:col + T], start=True, stop=True)
                last.then_inc(s_s, 1)

            def turn_probs(it, j, m):
                pe.wait_ge(s_pn, n_of(it, j, 2, m + 1))
                if m == 1 or not (isinstance(it, int) and it == 0 and j == 0):
                    pe.wait_ge(s_pt, n_of(it, j, 2, m))
                for i in range(4):
                    last = nc.tensor.transpose(PT[:, i * T:i * T + T], probs[:, m, i], id_sb[:, :])
                last.then_inc(s_t, 1)

            def values(it, j, m):
                pe.wait_ge(s_pt, n_of(it, j, 2, m + 1))
                if m == 0:
                    pe.wait_ge(s_vv, n_of(it, j, 2, 2))
                if m == 1 or not (isinstance(it, int) and it == 0 and j == 0):
                    pe.wait_ge(s_ol, n_of(it, j, 2, m))
                for b in range(2):
                    for h in range(HG):
                        col = (2 * h + b) * T
                        last = nc.tensor.matmul(OB[:, col:col + T], v_sb[:, j % 2, 2 * m + b, h * DH:h * DH + DH],
                                                probsT[:, m, HG * b + h], start=True, stop=True)
                last.then_inc(s_av, 1)

            def output(it, j):
                g, r = j % TG, (j % BODY) // TG
                if g == 0:
                    pe.wait_ge(s_wo, (BODY // TG) * it + (j // TG + 1))
                pe.wait_ge(s_ol, n_of(it, j, 2, 2))
                for c in range(KD):
                    if not (isinstance(it, int) and it == 0 and j == 0):
                        pe.wait_ge(s_acc, n_of(it, j, 2, c - 1) if c else n_of(it, j, 2, -1))
                    for h in range(HG):
                        last = exact(OP[c][:, :], lambda s: wo_hl[:, r, s, h, c * P:c * P + P],
                                     lambda s: o_hl[:, s, h, :], h == 0, h == HG - 1)
                    last.then_inc(s_op, 1)

            def first_half(it, j, more):
                scores(it, j, 0)
                if more:
                    project(it, j + 1, 0)
                scores(it, j, 1)

            def second_half(it, j, more):
                if more:
                    project(it, j + 1, 1)
                turn_probs(it, j, 0)
                if more:
                    project(it, j + 1, 2)
                values(it, j, 0)
                if more:
                    project(it, j + 1, 3)
                turn_probs(it, j, 1)
                if more:
                    project(it, j + 1, 4)
                values(it, j, 1)
                if more:
                    project(it, j + 1, 5)

            pe.wait_ge(s_x1l, KD * TG)
            for tile in range(6):
                project(0, 0, tile)
            first_half(0, 0, True)
            second_half(0, 0, True)
            first_half(0, 1, True)
            output(0, 0)
            with pe.Fori(0, NHG // 2 - 1) as it:
                for j in range(1, BODY + 1):
                    second_half(it, j, True)
                    first_half(it, j + 1, True)
                    output(it, j)
            it = NHG // 2 - 1
            for j in range(1, BODY):
                second_half(it, j, j < BODY - 1)
                if j < BODY - 1:
                    first_half(it, j + 1, j + 1 < BODY - 1)
                output(it, j)

            pe.wait_ge(s_w12, 2)
            for g in range(TG):
                pe.wait_ge(s_x2in, 16 * (g + 1))
                if g >= 1:
                    pe.wait_ge(s_mod, KD * (TG + g))
                turn_tokens(lambda b, c: x_tok2[:, b, c * P:c * P + P], bank[2:4]).then_inc(s_xt2, 1)
                pe.wait_ge(s_y, KD * (g + 1))
                if g >= 1:
                    pe.wait_ge(s_log, g)
                for b in range(BG):
                    for c in range(KD):
                        col = D * (b % 2) + P * c
                        last = nc.tensor.transpose(bank[4 + b // 2][:, col:col + P], yT[:, c, T * b:T * b + T],
                                                   id_sb[:, :])
                last.then_inc(s_yt, 1)
                pe.wait_ge(s_xhat, TG + g + 1)
                turn_tokens(lambda b, c: xhat2[:, b, c * P:c * P + P], bank[2:4]).then_inc(s_xT, 1)
                pe.wait_ge(s_x1l, KD * (TG + g + 1))
                if g:
                    pe.wait_ge(s_h, KD * g)

                def up(c):
                    k = F1 * g + c
                    if k >= 2:
                        pe.wait_ge(s_gel, k - 1)
                    for s in range(KD):
                        last = exact(bank[c % 2][:, :], lambda i: w1_hl[:, i, s, c * P:c * P + P],
                                     lambda i: x2_hl[:, i, s], s == 0, s == KD - 1)
                    last.then_inc(s_f1, 1)

                up(0)
                up(1)
                for c in range(F1):
                    if c + 2 < F1:
                        up(c + 2)
                    pe.wait_ge(s_fl, F1 * g + c + 1)
                    for m in range(KD):
                        last = exact(bank[6 + m][:, :], lambda i: w2_hl[:, i, c, m * P:m * P + P],
                                     lambda i: hid_hl[:, c % 4, i], c == 0, c == F1 - 1)
                last.then_inc(s_f2, 1)
                pe.wait_ge(s_h, KD * (g + 1))
                for b in range(BG):
                    for c in range(KD):
                        last = nc.tensor.matmul(bank[4][:, EG * b:EG * b + EG], hT[:, c, T * b:T * b + T],
                                                router_sb[:, c], start=c == 0, stop=c == KD - 1)
                last.then_inc(s_rl, 1)

            def gate_up(k0, g0, i):
                r, g, c = (i // (TG * CG)) % 2, (i // CG) % TG, i % CG
                if i % (TG * CG) == 0:
                    pe.wait_ge(s_wg, g0 + (i // (TG * CG) + 1))
                later = not (isinstance(k0, int) and k0 + i < 2)
                if later:
                    pe.wait_ge(s_sil, k0 + (i - 1))
                for o, banks in enumerate((GATE, UP)):
                    if o == 1 and later:
                        pe.wait_ge(s_hw, k0 + (i - 1))
                    for k in range(KD):
                        exact(banks[i % 2][:, :], lambda s: wgu_hl[r][:, s, k, c, o],
                              lambda s: tok_hl[:, s, k, N * g:N * g + N], k == 0, k == KD - 1)

            def combine(i):
                r, g, c = (i // (TG * CG)) % 2, (i // CG) % TG, i % CG
                nc.tensor.matmul(COMB[i % 2][:, :], sel_r[r][:, c], comb_r[0:SELK, N * g:N * g + N],
                                 start=True, stop=True).then_inc(s_g, 1)

            def down(k0, u0, i):
                r, c = (i // (TG * CG)) % 2, i % CG
                pe.wait_ge(s_hl3, k0 + (i + 1))
                if c == 0:
                    pe.wait_ge(s_da, KD * u0 + (KD * (i // CG) + 1))
                for m in range(KD):
                    last = exact(DOWN[m][:, :], lambda s: wd_hl[r][:, s, c, m * P:m * P + P],
                                 lambda s: hid_hl[:, i % 4, s], c == 0, c == CG - 1)
                if c == CG - 1:
                    last.then_inc(s_d, 1)

            pe.wait_ge(s_hl, KD * TG)
            for i in range(LAG):
                gate_up(0, 0, i)
            pe.wait_ge(s_comb, 1)
            pe.wait_ge(s_log, TG)
            for g in range(TG):
                if g >= 2:
                    pe.wait_ge(s_cl, g - 1)
                for b in range(BG):
                    last = nc.tensor.transpose(bank[4 + g % 2][0:EG, T * b:T * b + T], comb[:, BG * g + b], id_sb[:, :])
                last.then_inc(s_cT, 1)
            pe.wait_ge(s_cl, TG)
            for i in range(LAG):
                combine(i)
            body = 2 * TG * CG
            with pe.Fori(0, NCG // 2) as it:
                for i in range(body):
                    gate_up(body * it, 2 * it, i + LAG)
                    combine(i + LAG)
                    down(body * it, 2 * TG * it, i)
            k0, g0 = body * (NCG // 2), 2 * (NCG // 2)
            for i in range(TG * CG):
                if i + LAG < TG * CG:
                    gate_up(k0, g0, i + LAG)
                    combine(i + LAG)
                down(k0, g0 * TG, i)

            pe.wait_ge(s_hw, CH * TG)
            for g in range(TG):
                pe.wait_ge(s_da, KD * (TG * (NCG - 1) + g + 1) + 1)
                if g >= 2:
                    pe.wait_ge(s_fin, g - 1)
                for b in range(BG):
                    for c in range(KD):
                        col = D * (b % 2) + P * c
                        tok = N * g + T * b
                        last = nc.tensor.transpose(bank[2 * (g % 2) + b // 2][:, col:col + P], acc[:, c, tok:tok + T],
                                                   id_sb[:, :])
                last.then_inc(s_fT, 1)


def kernel(x, cond_2048, L0_cond_ada_w, L0_cond_ada_b, L0_cond_qkv_w, L0_cond_qkv_b, L0_cond_out_w, L0_cond_out_b,
           L0_cond_ffn_w1, L0_cond_ffn_b1, L0_cond_ffn_w2, L0_cond_ffn_b2, L0_ffn_router_w, L0_ffn_w_gate,
           L0_ffn_w_up, L0_ffn_w_down, L0_ffn_sh_gate, L0_ffn_sh_up, L0_ffn_sh_down, L0_ffn_sh_gate_w):
    import numpy as np
    import concourse.bacc as bacc
    from concourse.bass_utils import run_bass_kernel_spmd

    def a(v):
        return np.asarray(v)

    def by_slice(w):
        k, n = w.shape
        return w.reshape(k // P, P, n).transpose(1, 0, 2)

    def columns(b):
        return a(b).reshape(-1, P).T

    def hidden(experts, shared, axis):
        pad = np.zeros((CH * P - HID, D), np.float32)
        e = a(experts).transpose(1, 0, 2).reshape(D, E * I_MOE).T if axis == 2 else a(experts).reshape(E * I_MOE, D)
        s = a(shared).T if axis == 2 else a(shared)
        return np.concatenate([e, s, pad], 0)

    qkv = a(L0_cond_qkv_w).reshape(KD, P, 3, NHG, HG * DH).transpose(3, 1, 0, 2, 4)
    qkv_b = a(L0_cond_qkv_b).reshape(3, NHG, HG, DH)
    gate = hidden(L0_ffn_w_gate, L0_ffn_sh_gate, 2).reshape(NCG, CG, P, KD, P)
    up = hidden(L0_ffn_w_up, L0_ffn_sh_up, 2).reshape(NCG, CG, P, KD, P)
    gu = np.stack([gate, up], 0).transpose(1, 5, 4, 2, 0, 3)
    down = hidden(L0_ffn_w_down, L0_ffn_sh_down, 1).reshape(NCG, CG, P, D).transpose(0, 2, 1, 3)
    sel = np.zeros((SELK, CH * P), np.float32)
    for row in range(HID):
        e = min(row // I_MOE, E)
        sel[e, row] = sel[32 + e, row] = 1.0
    ins = {
        "x": a(x).reshape(B * T, D),
        "condT": a(cond_2048).T.reshape(KD, P, B).transpose(1, 0, 2),
        "ada_w": by_slice(a(L0_cond_ada_w)),
        "bias": np.concatenate([columns(L0_cond_ada_b), columns(L0_cond_out_b), columns(L0_cond_ffn_b1),
                                columns(L0_cond_ffn_b2)], 1),
        "bqk": qkv_b[0:2].transpose(1, 3, 0, 2).reshape(NHG, DH, 2 * HG),
        "bv": qkv_b[2].reshape(NHG, 1, HG * DH),
        "wqkv": qkv.reshape(NHG, P, KD, 3 * HG * DH),
        "wo": a(L0_cond_out_w).reshape(NHG, HG, DH, D).transpose(0, 2, 1, 3),
        "w1": by_slice(a(L0_cond_ffn_w1)),
        "w2": by_slice(a(L0_cond_ffn_w2)),
        "router": by_slice(np.concatenate([a(L0_ffn_router_w).T, a(L0_ffn_sh_gate_w)], 1)),
        "wgu": gu.reshape(NCG, P, KD * CG * 2 * P),
        "wd": down.reshape(NCG, P, CG * D),
        "sel": sel.reshape(SELK, NCG, CG * P).transpose(1, 0, 2),
        "ident": np.eye(P, dtype=np.float32),
    }
    nc = bacc.Bacc("TRN2", target_bir_lowering=False, num_devices=1)
    arrays, args = {}, []
    for name, v in ins.items():
        v = np.ascontiguousarray(v)
        arrays[f"in_{name}"] = v
        args.append(nc.dram_tensor(f"in_{name}", v.shape, mybir.dt.from_np(v.dtype), kind="ExternalInput").ap())
    args.append(nc.dram_tensor("out_y", (B * T, D), mybir.dt.float32, kind="ExternalOutput").ap())
    adaln_moe_kernel(nc, *args)
    r = run_bass_kernel_spmd(nc, [arrays], core_ids=[0])
    return r.results[0]["out_y"].reshape(B, T, D)
```

```python
import concourse.bass as bass
from concourse import mybir
from contextlib import ExitStack

B, T, D = 16, 128, 256
H, DH = 16, 128
MLP = 1024
E, TOPK, I_MOE, I_SH = 16, 4, 176, 704
P = 128
KD = D // P
N = 512
TG = B * T // N
BG = N // T
HG = 2
NHG = H // HG
UNITS = NHG * TG
BODY = 2 * TG
SCALE = DH ** -0.5
LN_EPS = 1e-6
F1 = MLP // P
HID = E * I_MOE + I_SH
CH = -(-HID // P)
CG = 4
NCG = CH // CG
EG = E + 1
SELK = 32 + EG
LAG = 2
FIN_LAG = (CG + 2, CG + 4)


def adaln_moe_kernel(nc, x, condT, ada_w, bias, bqk, bv, wqkv, wo, w1, w2, router, wgu, wd, sel, ident, out):
    f32 = mybir.dt.float32
    f32r = mybir.dt.float32r
    ALU = mybir.AluOpType
    ACT = mybir.ActivationFunctionType
    AX = mybir.AxisListType

    ADA_B, OUT_B, B1, B2 = 0, 12, 14, 22
    SHIFT1, SCALE1, GATE1, SHIFT2, SCALE2, GATE2 = 0, 2, 4, 6, 8, 10

    x_tok_view = x.rearrange("(g b t) d -> g t b d", b=BG, t=T)
    out_view = out.rearrange("(g b t) d -> g t b d", b=BG, t=T)

    with ExitStack() as ctx:
        def sb(name, shape, dt=f32):
            return ctx.enter_context(nc.sbuf_tensor(name, shape, dt))

        def sem(name):
            return ctx.enter_context(nc.semaphore(name))

        arena_a = sb("arena_a", [P, 10240], f32r)
        arena_b = sb("arena_b", [P, 8192], f32r)
        tok_hl = sb("tok_hl", [P, 2, KD, B * T], f32r)
        x2_hl = sb("x2_hl", [P, 2, 2, KD, N], f32r)
        hid_hl = sb("hid_hl", [P, 4, 2, N], f32r)
        wqkv_hl = arena_a[:, 0:6144].rearrange("p (r s k n) -> p r s k n", r=2, s=2, k=KD)
        wo_hl = arena_a[:, 6144:8192].rearrange("p (r s h n) -> p r s h n", r=2, s=2, h=HG)
        o_hl = arena_a[:, 8192:10240].rearrange("p (s h n) -> p s h n", s=2, h=HG)
        w1_hl = arena_b[:, 0:4096].rearrange("p (s k n) -> p s k n", s=2, k=KD)
        w2_hl = arena_b[:, 4096:8192].rearrange("p (s k n) -> p s k n", s=2, k=F1)
        wgu_hl = [a[:, 0:4096].rearrange("p (s k c g n) -> p s k c g n", s=2, k=KD, c=CG, g=2) for a in (arena_a, arena_b)]
        wd_hl = [a[:, 4096:6144].rearrange("p (s c n) -> p s c n", s=2, c=CG) for a in (arena_a, arena_b)]
        sel_r = [arena_a[0:SELK, o:o + CG * P].rearrange("p (c n) -> p c n", c=CG) for o in (6144, 6144 + CG * P)]
        comb_r = arena_a[:, 7168:9216]

        acc = sb("acc", [P, KD, B * T])
        raw = sb("raw", [P, 4096])
        bv_sb = sb("bv_sb", [P, 2, HG * DH])
        bqk_sb = sb("bqk_sb", [P, 2, 2 * HG])
        work = sb("work", [P, 8192])
        ada_sb = sb("ada_sb", [P, 12, B])
        bias_sb = sb("bias_sb", [P, 24])
        cond_sb = sb("cond_sb", [P, KD, B])
        router_sb = sb("router_sb", [P, KD, EG])
        id_sb = sb("id_sb", [P, P])
        stats = sb("stats", [P, BG, 6])
        mv = sb("mv", [P, 2, BG, 2])
        veps = sb("veps", [P, 2, BG])
        rstd = sb("rstd", [P, 2, BG])
        mhalf = sb("mhalf", [P, BG])
        ones = sb("ones", [P, 1])
        rmax = sb("rmax", [P, 2, BG])
        negm = sb("negm", [P, 2, BG])
        rsum = sb("rsum", [P, 2, BG])
        rinv = sb("rinv", [P, 2, BG])

        ada_w_sb = acc[:, :, 0:1536]
        def slot(where, first, d=D):
            return where[:, first:first + 1024].rearrange("p (b d) -> p b d", d=d)
        x_in = [slot(work, 1024), slot(work, 3072)]
        xhat1 = [slot(work, 6144), slot(work, 7168)]
        mod1 = [slot(work, 5120, N), acc[:, :, 1536:2048]]
        raw_qkv = [raw[:, r * 2048:r * 2048 + 1536].rearrange("p (k n) -> p k n", k=KD) for r in range(2)]
        raw_o = [raw[:, r * 2048 + 1536:r * 2048 + 2048].rearrange("p (h n) -> p h n", h=HG) for r in range(2)]
        qT = work[:, 0:2048].rearrange("p (r h n) -> p r h n", r=2, h=HG)
        kT = work[:, 2048:4096].rearrange("p (r h n) -> p r h n", r=2, h=HG)
        v_sb = work[:, 4096:6144].rearrange("p (r b n) -> p r b n", r=2, b=BG)
        probs = work[:, 6144:7168].rearrange("p (r j n) -> p r j n", r=2, j=4)
        probsT = work[:, 7168:8192].rearrange("p (r j n) -> p r j n", r=2, j=4)
        raw_w1 = raw[:, 0:2048].rearrange("p (k n) -> p k n", k=KD)
        raw_w2 = raw[:, 2048:4096].rearrange("p (k n) -> p k n", k=F1)
        raw_gu, raw_d, raw_sel = [[a[0:n, o + f:o + f + w] for a, o in ((work, 4096), (raw, 0))]
                                  for n, f, w in ((P, 0, 2048), (P, 2048, 1024), (SELK, 3072, CG * P))]
        x_tok2, xhat2, mod2 = slot(raw, 0), slot(raw, 1024), slot(raw, 2048, N)
        yT = [slot(raw, 3072, N), slot(work, 0, N)]
        hT, part, gel = slot(work, 1024, N), slot(work, 2048, N), slot(work, 3072, N)
        def rt(i, n):
            return work[:, 4096 + 512 * i:4096 + 512 * i + B * n].rearrange("p (b e) -> p b e", b=B)
        logits = sb("logits", [P, B, EG])
        shifted, expd, pr, top, rest, comb = rt(0, E), rt(1, EG), rt(2, E), rt(3, 8), rt(4, E), rt(5, EG)
        r_small = work[:, 4096 + 512 * 6:8192].rearrange("p (i b) -> p i b", b=B)
        sil = work[:, 2048:3072].rearrange("p (r n) -> p r n", r=2)
        gu = work[:, 3072:4096].rearrange("p (r n) -> p r n", r=2)
        hw = work[:, 0:1024].rearrange("p (r n) -> p r n", r=2)
        x_fin = work[:, 4096:6144].rearrange("p (r b d) -> p r b d", r=2, b=BG)
        y_fin = work[:, 6144:8192].rearrange("p (r b d) -> p r b d", r=2, b=BG)

        bank = [ctx.enter_context(nc.psum_tensor(f"bank{i}", [P, N], f32)) for i in range(8)]
        PROJ, SC, PT, OB, OP = bank[0:2], bank[2:4], bank[4], bank[5], bank[6:8]
        GATE, UP, COMB, SPARE, DOWN = bank[0:2], bank[2:4], bank[4], bank[5], bank[6:8]

        LOGITS = [bank[4], bank[4], bank[4], bank[6]]

        s_load = sem("s_load")
        s_aw = [sem("s_aw0"), sem("s_aw1")]
        s_rw = sem("s_rw")
        s_x = [sem("s_x0"), sem("s_x1")]
        s_raw = [sem("s_raw0"), sem("s_raw1")]
        s_w1raw, s_w2raw = sem("s_w1raw"), sem("s_w2raw")
        s_graw = sem("s_graw")
        s_pool = sem("s_pool")
        s_act = sem("s_act")
        s_v = sem("s_v")
        s_ada_mm = sem("s_ada_mm")
        s_ada = sem("s_ada")
        s_var = sem("s_var")
        s_rstd = sem("s_rstd")
        s_xhat = sem("s_xhat")
        s_xT = sem("s_xT")
        s_mod = sem("s_mod")
        s_x1h = sem("s_x1h")
        s_x1l = sem("s_x1l")
        s_wq = sem("s_wq")
        s_wo = sem("s_wo")
        s_pj = sem("s_pj")
        s_qk = sem("s_qk")
        s_vv = sem("s_vv")
        s_s = sem("s_s")
        s_negm = sem("s_negm")
        s_exp = sem("s_exp")
        s_pn = sem("s_pn")
        s_t = sem("s_t")
        s_pt = sem("s_pt")
        s_av = sem("s_av")
        s_oh = sem("s_oh")
        s_ol = sem("s_ol")
        s_op = sem("s_op")
        s_acc = sem("s_acc")
        s_clr = sem("s_clr")
        s_w12 = sem("s_w12")
        s_xt2 = sem("s_xt2")
        s_x2in = sem("s_x2in")
        s_y = sem("s_y")
        s_yt = sem("s_yt")
        s_f1 = sem("s_f1")
        s_gel = sem("s_gel")
        s_fh = sem("s_fh")
        s_fl = sem("s_fl")
        s_f2 = sem("s_f2")
        s_h = sem("s_h")
        s_hh = sem("s_hh")
        s_rl = sem("s_rl")
        s_log = sem("s_log")
        s_re = sem("s_re")
        s_rx = sem("s_rx")
        s_comb = sem("s_comb")
        s_cT = sem("s_cT")
        s_ch = sem("s_ch")
        s_cl = sem("s_cl")
        s_wgu = sem("s_wgu")
        s_wdn = sem("s_wdn")
        s_wg = sem("s_wg")
        s_t1 = sem("s_t1")
        s_hl = sem("s_hl")
        s_czero = sem("s_czero")
        s_gu = sem("s_gu")
        s_g = sem("s_g")
        s_sil = sem("s_sil")
        s_hw = sem("s_hw")
        s_hh3 = sem("s_hh3")
        s_hl3 = sem("s_hl3")
        s_d = sem("s_d")
        s_da = sem("s_da")
        s_xf = [sem("s_xf0"), sem("s_xf1")]
        s_fT = sem("s_fT")
        s_fin = sem("s_fin")
        s_out = [sem("s_out0"), sem("s_out1")]

        PARTS = ((0, 0), (0, 1), (1, 0))

        block = ctx.enter_context(nc.Block())

        def flat(ap):
            dims = " ".join("abcd"[:len(ap.shape) - 1])
            return ap.rearrange(f"p {dims} -> p ({dims})")

        def split(eng, halves, whole, done, own):
            hi, lo, whole = flat(halves[:, 0]), flat(halves[:, 1]), flat(whole)
            eng.tensor_tensor(hi, whole, ones[:, 0:1].to_broadcast(whole.shape), ALU.mult).then_inc(s_pool, 1)
            eng.wait_ge(s_pool, own)
            eng.tensor_tensor(lo, whole, hi.bitcast(f32), ALU.subtract).then_inc(done, 1)

        @block.sync
        def _(sp):
            def load_x(g):
                sp.dma_start(x_in[g % 2], x_tok_view[g]).then_inc(s_x[g % 2], 16)

            sp.dma_start(id_sb[:, :], ident).then_inc(s_load, 16)
            sp.dma_start(cond_sb[:, :, :], condT).then_inc(s_load, 16)
            sp.dma_start(bias_sb[:, :], bias).then_inc(s_load, 16)
            load_x(0)
            sp.dma_start(ada_w_sb[:, :, 0:512], ada_w[:, :, 0:512]).then_inc(s_aw[0], 16)

            def load_heads(hg, r):
                sp.dma_start(raw_qkv[r], wqkv[hg]).then_inc(s_raw[r], 16)
                sp.dma_start(raw_o[r], wo[hg]).then_inc(s_raw[r], 16)
                sp.dma_start(bqk_sb[:, r], bqk[hg]).then_inc(s_raw[r], 16)
                sp.dma_start(bv_sb[:, r], bv[hg].to_broadcast([P, HG * DH])).then_inc(s_raw[r], 16)

            def load_group(g, r=1):
                sp.dma_start(raw_gu[r], wgu[g]).then_inc(s_graw, 16)
                sp.dma_start(raw_d[r], wd[g]).then_inc(s_graw, 16)
                sp.dma_start(raw_sel[r], sel[g]).then_inc(s_graw, 16)

            load_heads(0, 0)
            load_x(1)
            sp.dma_start(ada_w_sb[:, :, 512:1536], ada_w[:, :, 512:1536]).then_inc(s_aw[1], 16)
            for g in range(2, TG):
                sp.wait_ge(s_xhat, g - 1)
                load_x(g)
            load_heads(1, 1)
            sp.dma_start(router_sb[:, :, :], router).then_inc(s_rw, 16)
            with sp.Fori(1, NHG // 2) as it:
                for r in range(2):
                    sp.wait_ge(s_wo, 2 * it + (r - 1))
                    sp.wait_ge(s_vv, 16 * it + (8 * r - 8))
                    load_heads(2 * it + r, r)
            sp.wait_ge(s_wo, NHG)
            sp.dma_start(raw_w1, w1).then_inc(s_w1raw, 16)
            sp.dma_start(raw_w2, w2).then_inc(s_w2raw, 16)
            sp.wait_ge(s_w12, 2)
            sp.dma_start(x_tok2, x_tok_view[0]).then_inc(s_x2in, 16)
            sp.wait_ge(s_acc, KD * UNITS)
            load_group(0, 0)
            for g in range(1, TG):
                sp.wait_ge(s_xt2, g)
                sp.dma_start(x_tok2, x_tok_view[g]).then_inc(s_x2in, 16)
            sp.wait_ge(s_h, KD * TG)
            load_group(1)
            with sp.Fori(2, NCG) as g:
                sp.wait_ge(s_wg, g)
                load_group(g)
            sp.wait_ge(s_cT, TG)
            for g in range(TG):
                if g >= 2:
                    sp.wait_ge(s_fin, 2 * (g - 1))
                sp.dma_start(x_fin[:, g % 2], x_tok_view[g]).then_inc(s_xf[g % 2], 16)
                if g >= 1:
                    sp.wait_ge(s_fin, 2 * g)
                    sp.dma_start(out_view[g - 1], y_fin[:, (g - 1) % 2]).then_inc(s_out[(g - 1) % 2], 16)
            sp.wait_ge(s_fin, 2 * TG)
            sp.dma_start(out_view[TG - 1], y_fin[:, (TG - 1) % 2]).then_inc(s_out[(TG - 1) % 2], 16)
            sp.wait_ge(s_out[0], 16 * TG // 2)
            sp.wait_ge(s_out[1], 16 * TG // 2)

        def split_group(eng, r, own, staged=1):
            split(eng, wgu_hl[r], raw_gu[staged].rearrange("p (k c g n) -> p k c g n", k=KD, c=CG, g=2), s_wgu, own)
            split(eng, wd_hl[r], raw_d[staged].rearrange("p (c n) -> p c n", c=CG), s_wdn, own + 1)
            eng.tensor_copy(sel_r[r], raw_sel[staged].rearrange("p (c n) -> p c n", c=CG)).then_inc(s_wg, 1)

        @block.gpsimd
        def _(pool):
            pool.memset(mhalf[:, :], -0.5).then_inc(s_pool, 1)
            pool.memset(ones[:, :], 1.0).then_inc(s_pool, 1)
            own = 2

            def inverse_root(g, r, own):
                pool.wait_ge(s_var, g + 1)
                pool.tensor_scalar(veps[:, r], mv[:, r, :, 1], LN_EPS, None, ALU.add).then_inc(s_pool, 1)
                pool.wait_ge(s_pool, own + 1)
                pool.tensor_tensor(rstd[:, r], veps[:, r], mhalf[:, :], ALU.pow).then_inc(s_rstd, 1)
                return own + 1

            for g in range(TG):
                if g >= 2:
                    pool.wait_ge(s_xhat, g - 1)
                own = inverse_root(g, g % 2, own)
                if g == 0:
                    pool.wait_ge(s_raw[0], 64)
                    split(pool, wqkv_hl[:, 0], raw_qkv[0], s_wq, own + 1)
                    own += 1
            split(pool, wo_hl[:, 0], raw_o[0], s_wo, own + 1)
            pool.wait_ge(s_ada_mm, 2)
            pool.wait_ge(s_x1l, KD * TG)
            pool.memset(acc[:, :, :], 0.0).then_inc(s_clr, 1)
            pool.wait_ge(s_raw[1], 64)
            split(pool, wqkv_hl[:, 1], raw_qkv[1], s_wq, own + 2)
            split(pool, wo_hl[:, 1], raw_o[1], s_wo, own + 3)
            own += 3
            with pool.Fori(1, NHG // 2) as it:
                for r in range(2):
                    pool.wait_ge(s_raw[r], 64 * it + 64)
                    pool.wait_ge(s_pj, 48 * it + (24 * r - 24))
                    split(pool, wqkv_hl[:, r], raw_qkv[r], s_wq, 4 * it + (own - 4 + 2 * r + 1))
                    pool.wait_ge(s_op, 16 * it + (8 * r - 8))
                    split(pool, wo_hl[:, r], raw_o[r], s_wo, 4 * it + (own - 4 + 2 * r + 2))
            own += 4 * (NHG // 2 - 1)
            pool.wait_ge(s_w1raw, 16)
            split(pool, w1_hl, raw_w1, s_w12, own + 1)
            pool.wait_ge(s_w2raw, 16)
            split(pool, w2_hl, raw_w2, s_w12, own + 2)
            own += 2
            for g in range(TG):
                own = inverse_root(TG + g, g % 2, own)
                if g == 1:
                    pool.wait_ge(s_graw, 48)
                    split_group(pool, 0, own + 1, staged=0)
                    own += 2
            pool.wait_ge(s_t1, KD * TG)
            pool.memset(acc[:, :, :], 0.0).then_inc(s_clr, 1)
            pool.wait_ge(s_graw, 96)
            pool.wait_ge(s_f2, TG)
            split_group(pool, 1, own + 1)
            own += 2
            with pool.Fori(1, NCG // 2) as it:
                for r in range(2):
                    pool.wait_ge(s_graw, 96 * it + (48 * r + 48))
                    pool.wait_ge(s_d, 8 * it + (4 * r - 4))
                    split_group(pool, r, 4 * it + (own - 4 + 2 * r + 1))
            own += 4 * (NCG // 2 - 1)
            pool.wait_ge(s_graw, 48 * NCG)
            pool.wait_ge(s_d, TG * (NCG - 2))
            split_group(pool, 0, own + 1)

        def n_of(it, j, per, c):
            return per * BODY * it + (per * j + c)

        @block.scalar
        def _(act):
            def modulate(q, g, c, turned, target, scale, shift, high):
                for b in range(BG):
                    at = BG * g + b
                    last = nc.scalar.activation(target[:, c, b * T:b * T + T], turned[c][:, b * T:b * T + T],
                                                ACT.Identity, scale=ada_sb[:, scale + c, at:at + 1],
                                                bias=ada_sb[:, shift + c, at:at + 1])
                last.then_inc(s_mod, 1)
                act.wait_ge(s_mod, KD * q + c + 1)
                nc.scalar.activation(high, target[:, c], ACT.Copy).then_inc(s_x1h, 1)

            def prologue(g, c):
                if c == 0:
                    act.wait_ge(s_xT, g + 1)
                    if g >= 2:
                        act.wait_ge(s_x1l, KD * (g - 1))
                modulate(g, g, c, bank[2 + 2 * (g % 2):4 + 2 * (g % 2)], mod1[g % 2], SCALE1, SHIFT1,
                         tok_hl[:, 0, c, N * g:N * g + N])

            def project(it, j, tile):
                act.wait_ge(s_pj, n_of(it, j, 6, tile + 1))
                dst = (qT if tile < HG else kT)[:, j % 2, tile % HG]
                r = (j % BODY) // TG
                nc.scalar.activation(dst, PROJ[tile % 2][:, :], ACT.Identity,
                                     bias=bqk_sb[:, r, tile:tile + 1]).then_inc(s_qk, 1)

            def attend(it, j, more):
                for m in range(2):
                    act.wait_ge(s_negm, n_of(it, j, 2, m + 1))
                    for i in range(4):
                        last = nc.scalar.activation(probs[:, m, i], SC[m][:, i * T:i * T + T], ACT.Exp,
                                                    bias=negm[:, m, i:i + 1], scale=SCALE,
                                                    accum_out=rsum[:, m, i:i + 1])
                    last.then_inc(s_exp, 1)
                    if more:
                        project(it, j + 1, m)
                for m in range(2):
                    act.wait_ge(s_t, n_of(it, j, 2, m + 1))
                    nc.scalar.activation(probsT[:, m], PT[:, :].rearrange("p (i n) -> p i n", i=4), ACT.Copy)\
                        .then_inc(s_pt, 1)
                    if more:
                        project(it, j + 1, 2 + m)
                    act.wait_ge(s_av, n_of(it, j, 2, m + 1))
                    nc.scalar.activation(o_hl[:, 0, :, 256 * m:256 * m + 256],
                                         OB[:, :].rearrange("p (h n) -> p h n", h=HG), ACT.Copy).then_inc(s_oh, 1)

            act.wait_ge(s_ada, 1)
            prologue(0, 0)
            prologue(0, 1)
            act.wait_ge(s_raw[0], 64)
            project(0, 0, 0)
            project(0, 0, 1)
            prologue(1, 0)
            project(0, 0, 2)
            project(0, 0, 3)
            prologue(1, 1)
            for g in range(2, TG):
                for c in range(KD):
                    prologue(g, c)
            with act.Fori(0, NHG // 2 - 1) as it:
                for j in range(BODY):
                    if j == TG - 1:
                        act.wait_ge(s_raw[1], 64 * it + 64)
                    if j == BODY - 1:
                        act.wait_ge(s_raw[0], 64 * it + 128)
                    attend(it, j, True)
            for j in range(BODY):
                if j == TG - 1:
                    act.wait_ge(s_raw[1], 64 * NHG // 2)
                attend(NHG // 2 - 1, j, j < BODY - 1)

            def second_norm(g):
                act.wait_ge(s_xT, TG + g + 1)
                if g >= 1:
                    act.wait_ge(s_x1l, KD * (TG + g))
                for c in range(KD):
                    modulate(TG + g, g, c, bank[0:2] if g == 0 else bank[2:4], mod2, SCALE2, SHIFT2,
                             x2_hl[:, g % 2, 0, c])

            def high_h(g):
                for c in range(KD):
                    act.wait_ge(s_h, KD * g + c + 1)
                    nc.scalar.activation(tok_hl[:, 0, c, N * g:N * g + N], hT[:, c], ACT.Copy).then_inc(s_hh, 1)

            def exponentials(part, b0, b1):
                act.wait_ge(s_re, part)
                nc.scalar.activation(expd[:, b0:b1, 0:E], shifted[:, b0:b1], ACT.Exp)
                nc.scalar.activation(expd[:, b0:b1, E:EG], logits[:, b0:b1, E:EG], ACT.Exp, scale=-1.0)\
                    .then_inc(s_rx, 1)

            second_norm(0)
            for g in range(TG):
                for c in range(F1):
                    k = F1 * g + c
                    act.wait_ge(s_f1, k + 1)
                    if k >= 2:
                        act.wait_ge(s_fl, k - 1)
                    nc.scalar.activation(gel[:, c % 2], bank[c % 2][:, :], ACT.Gelu,
                                         bias=bias_sb[:, B1 + c:B1 + c + 1]).then_inc(s_gel, 1)
                    act.wait_ge(s_gel, k + 1)
                    nc.scalar.activation(hid_hl[:, c % 4, 0], gel[:, c % 2], ACT.Copy).then_inc(s_fh, 1)
                    if g >= 1 and c == 1:
                        high_h(g - 1)
                if g + 1 < TG:
                    second_norm(g + 1)
            exponentials(1, 0, B - BG)
            act.wait_ge(s_czero, 1)

            def high_comb(g):
                act.wait_ge(s_cT, g + 1)
                nc.scalar.activation(comb_r[0:EG, N * g:N * g + N], bank[4 + g % 2][0:EG, :], ACT.Copy)\
                    .then_inc(s_ch, 1)

            for g in range(TG - 2):
                high_comb(g)
            high_h(TG - 1)
            exponentials(2, B - BG, B)
            for g in range(TG - 2, TG):
                high_comb(g)

            def chunk(k0, i):
                act.wait_ge(s_g, k0 + (i + 1))
                nc.scalar.activation(sil[:, i % 2], GATE[i % 2][:, :], ACT.Silu).then_inc(s_sil, 1)
                act.wait_ge(s_hw, k0 + (i + 1))
                nc.scalar.activation(hid_hl[:, i % 4, 0], hw[:, i % 2], ACT.Copy).then_inc(s_hh3, 1)

            with act.Fori(0, NCG // 2) as it:
                for i in range(2 * TG * CG):
                    chunk(2 * TG * CG * it, i)
            for i in range(TG * CG):
                chunk(2 * TG * CG * (NCG // 2), i)

        @block.vector
        def _(dve):
            own = 0

            def modulation(first, many, own):
                wide = nc.vector.tensor_tensor(
                    ada_sb[:, first:first + many],
                    bank[6 + first // 4 % 2][:, 0:many * B].rearrange("p (c b) -> p c b", b=B),
                    bias_sb[:, ADA_B + first:ADA_B + first + many].unsqueeze(2).to_broadcast([P, many, B]), ALU.add)
                wide.then_inc(s_v, 1)
                dve.wait_ge(s_v, own + 1)
                c = SCALE1 if first == 0 else SCALE2
                nc.vector.tensor_scalar(ada_sb[:, c:c + KD], ada_sb[:, c:c + KD], 1.0, None, ALU.add)\
                    .then_inc(s_ada, 1)
                return own + 1

            def ada_of(c, g):
                return ada_sb[:, c, BG * g:BG * g + BG].unsqueeze(2).to_broadcast([P, BG, T])

            def by_batch(ap):
                return ap.rearrange("p (b t) -> p b t", b=BG)

            def statistics(source, r, own):
                for b in range(BG):
                    nc.vector.bn_stats(out=stats[:, b], in_=source(b)).then_inc(s_v, 1)
                dve.wait_ge(s_v, own + BG)
                for b in range(BG):
                    last = nc.vector.bn_aggr(out=mv[:, r, b], in_=stats[:, b])
                last.then_inc(s_var, 1)
                return own + BG

            def normalise(g, source, target, r):
                dve.wait_ge(s_rstd, g + 1)
                for b in range(BG):
                    last = nc.vector.tensor_scalar(target[:, b], source(b), mv[:, r, b, 0:1], rstd[:, r, b:b + 1],
                                                   ALU.subtract, ALU.mult)
                last.then_inc(s_xhat, 1)

            def low_half(target, whole, high):
                return nc.vector.tensor_tensor(target, whole, high.bitcast(f32), ALU.subtract)

            def normalise1(g, own):
                dve.wait_ge(s_x[g % 2], 16 * (g // 2 + 1))
                own = statistics(lambda b: x_in[g % 2][:, b], g % 2, own)
                if g >= 2:
                    dve.wait_ge(s_xT, g - 1)
                normalise(g, lambda b: x_in[g % 2][:, b], xhat1[g % 2], g % 2)
                return own

            def low1(g):
                for c in range(KD):
                    dve.wait_ge(s_x1h, KD * g + c + 1)
                    low_half(tok_hl[:, 1, c, N * g:N * g + N], mod1[g % 2][:, c], tok_hl[:, 0, c, N * g:N * g + N])\
                        .then_inc(s_x1l, 1)

            own = normalise1(0, own)
            dve.wait_ge(s_load, 48)
            dve.wait_ge(s_ada_mm, 1)
            own = modulation(0, 4, own)
            own = normalise1(1, own)
            low1(0)
            own = normalise1(2, own)

            def head(it, j, base):
                for m in range(2):
                    dve.wait_ge(s_s, n_of(it, j, 2, m + 1))
                    nc.vector.tensor_reduce(rmax[:, m], SC[m][:, :].rearrange("p (i n) -> p i n", i=4), AX.X, ALU.max)\
                        .then_inc(s_v, 1)
                    dve.wait_ge(s_v, n_of(it, j, 4, base + m + 1))
                    nc.vector.tensor_scalar(negm[:, m], rmax[:, m], -SCALE, None, ALU.mult).then_inc(s_negm, 1)
                normal(it, j, base, 0)

            def normal(it, j, base, m):
                dve.wait_ge(s_exp, n_of(it, j, 2, m + 1))
                nc.vector.reciprocal(rinv[:, m], rsum[:, m]).then_inc(s_v, 1)
                dve.wait_ge(s_v, n_of(it, j, 4, base + 3 + m))
                nc.vector.tensor_tensor(probs[:, m], probs[:, m], rinv[:, m].unsqueeze(2).to_broadcast([P, 4, T]),
                                        ALU.mult).then_inc(s_pn, 1)

            def add_projection(it, j):
                g = j % TG
                for m in range(KD):
                    dve.wait_ge(s_op, n_of(it, j, 2, m + 1))
                    here = acc[:, m, N * g:N * g + N]
                    nc.vector.tensor_tensor(here, OP[m][:, :], here, ALU.add).then_inc(s_acc, 1)

            def project_v(it, j, tile):
                dve.wait_ge(s_pj, n_of(it, j, 6, 4 + tile + 1))
                r = (j % BODY) // TG
                nc.vector.tensor_tensor(v_sb[:, j % 2, 2 * tile:2 * tile + 2],
                                        PROJ[tile][:, :].rearrange("p (b n) -> p b n", b=2),
                                        bv_sb[:, r].unsqueeze(1).to_broadcast([P, 2, HG * DH]), ALU.add)\
                    .then_inc(s_vv, 1)

            def low_o(it, j, m):
                dve.wait_ge(s_oh, n_of(it, j, 2, m + 1))
                low_half(o_hl[:, 1, :, 256 * m:256 * m + 256], OB[:, :].rearrange("p (h n) -> p h n", h=HG),
                         o_hl[:, 0, :, 256 * m:256 * m + 256]).then_inc(s_ol, 1)

            def tail(it, j, base, more):
                normal(it, j, base, 1)
                for m in range(2):
                    low_o(it, j, m)
                    if more:
                        project_v(it, j + 1, m)

            low1(1)
            dve.wait_ge(s_raw[0], 64)
            for tile in range(2):
                project_v(0, 0, tile)
            own = normalise1(3, own)
            low1(2)
            low1(3)
            dve.wait_ge(s_ada_mm, 2)
            own = modulation(4, 8, own)
            dve.wait_ge(s_clr, 1)
            base = own
            head(0, 0, base)
            with dve.Fori(0, NHG // 2 - 1) as it:
                for j in range(BODY):
                    if j == TG - 1:
                        dve.wait_ge(s_raw[1], 64 * it + 64)
                    if j == BODY - 1:
                        dve.wait_ge(s_raw[0], 64 * it + 128)
                    tail(it, j, base, True)
                    head(it, j + 1, base)
                    add_projection(it, j)
            def gated_attention(g):
                if g >= 2:
                    dve.wait_ge(s_h, KD * (g - 1))
                for c in range(KD):
                    nc.vector.scalar_tensor_tensor(out=by_batch(yT[g % 2][:, c]),
                                                   in0=by_batch(acc[:, c, N * g:N * g + N]),
                                                   scalar=bias_sb[:, OUT_B + c:OUT_B + c + 1], in1=ada_of(GATE1 + c, g),
                                                   op0=ALU.add, op1=ALU.mult).then_inc(s_t1, 1)

            def residual(g):
                dve.wait_ge(s_t1, KD * (g + 1))
                dve.wait_ge(s_xt2, g + 1)
                for c in range(KD):
                    turned = bank[c if g == 0 else 2 + c]
                    nc.vector.tensor_tensor(yT[g % 2][:, c], turned[:, :], yT[g % 2][:, c], ALU.add).then_inc(s_y, 1)

            def source(g):
                return lambda b: bank[b // 2 if g == 0 else 4 + b // 2][:, D * (b % 2):D * (b % 2) + D]

            def statistics2(g, own):
                dve.wait_ge(s_yt, g + 1)
                return statistics(source(g), g % 2, own)

            def normalise2(g):
                normalise(TG + g, source(g), xhat2, g % 2)

            def low2(g):
                for c in range(KD):
                    dve.wait_ge(s_x1h, KD * (TG + g) + c + 1)
                    low_half(x2_hl[:, g % 2, 1, c], mod2[:, c], x2_hl[:, g % 2, 0, c]).then_inc(s_x1l, 1)

            it = NHG // 2 - 1
            for j in range(BODY - 1):
                if j == TG - 1:
                    dve.wait_ge(s_raw[1], 64 * NHG // 2)
                tail(it, j, base, True)
                head(it, j + 1, base)
                if j == BODY - 2:
                    dve.wait_ge(s_acc, KD * (UNITS - TG + 1))
                    dve.wait_ge(s_w12, 2)
                    gated_attention(0)
                add_projection(it, j)
            own += 4 * UNITS
            j = BODY - 1
            normal(it, j, base, 1)
            residual(0)
            low_o(it, j, 0)
            own = statistics2(0, own)
            low_o(it, j, 1)
            normalise2(0)
            add_projection(it, j)
            dve.wait_ge(s_acc, KD * UNITS)
            low2(0)

            def step(ins, own):
                ins.then_inc(s_v, 1)
                dve.wait_ge(s_v, own + 1)
                return own + 1

            def shift_logits(b0, b1, own):
                dve.wait_ge(s_log, b1 // BG)
                own = step(nc.vector.tensor_reduce(r_small[:, 0, b0:b1], logits[:, b0:b1, 0:E], AX.X, ALU.max), own)
                nc.vector.tensor_tensor(shifted[:, b0:b1], logits[:, b0:b1, 0:E],
                                        r_small[:, 0, b0:b1].unsqueeze(2).to_broadcast([P, b1 - b0, E]), ALU.subtract)\
                    .then_inc(s_re, 1)
                return own

            def combine_weights(part, b0, b1, own):
                def small(i):
                    return r_small[:, i, b0:b1]

                def along(ap):
                    return ap.unsqueeze(2).to_broadcast([P, b1 - b0, E])

                some = slice(b0, b1)
                dve.wait_ge(s_rx, part)
                own = step(nc.vector.tensor_reduce(small(1), expd[:, some, 0:E], AX.X, ALU.add), own)
                nc.vector.tensor_scalar(small(6), expd[:, some, E], 1.0, None, ALU.add).then_inc(s_v, 1)
                own = step(nc.vector.reciprocal(small(2), small(1)), own + 1)
                nc.vector.reciprocal(comb[:, some, E], small(6)).then_inc(s_v, 1)
                own = step(nc.vector.tensor_tensor(pr[:, some], expd[:, some, 0:E], along(small(2)), ALU.mult), own + 1)
                for b in range(b0, b1):
                    last = nc.vector.max(out=top[:, b], in_=pr[:, b])
                own = step(last, own)
                own = step(nc.vector.tensor_reduce(small(3), top[:, some, 0:TOPK], AX.X, ALU.add), own)
                nc.vector.memset(top[:, some, TOPK:8], -1.0).then_inc(s_v, 1)
                own = step(nc.vector.tensor_scalar(small(4), small(3), 1e-9, None, ALU.max), own + 1)
                nc.vector.reciprocal(small(5), small(4)).then_inc(s_v, 1)
                for b in range(b0, b1):
                    last = nc.vector.match_replace(out=rest[:, b], in_to_replace=top[:, b], in_values=pr[:, b],
                                                   imm_value=0.0)
                own = step(last, own + 1)
                own = step(nc.vector.tensor_tensor(pr[:, some], pr[:, some], rest[:, some], ALU.subtract), own)
                nc.vector.tensor_tensor(comb[:, some, 0:E], pr[:, some], along(small(5)), ALU.mult).then_inc(s_comb, 1)
                return own

            def low_comb(g):
                dve.wait_ge(s_ch, g + 1)
                low_half(comb_r[32:32 + EG, N * g:N * g + N], bank[4 + g % 2][0:EG, :],
                         comb_r[0:EG, N * g:N * g + N]).then_inc(s_cl, 1)

            def make_h(g, own):
                dve.wait_ge(s_f2, g + 1)
                for c in range(KD):
                    nc.vector.scalar_tensor_tensor(out=by_batch(part[:, c]), in0=by_batch(DOWN[c][:, :]),
                                                   scalar=bias_sb[:, B2 + c:B2 + c + 1], in1=ada_of(GATE2 + c, g),
                                                   op0=ALU.add, op1=ALU.mult).then_inc(s_v, 1)
                if g >= 1:
                    dve.wait_ge(s_rl, g)
                for c in range(KD):
                    dve.wait_ge(s_v, own + c + 1)
                    nc.vector.tensor_tensor(hT[:, c], part[:, c], yT[g % 2][:, c], ALU.add).then_inc(s_h, 1)
                return own + KD

            def low_h(g):
                for c in range(KD):
                    dve.wait_ge(s_hh, KD * g + c + 1)
                    cols = slice(N * g, N * g + N)
                    low_half(tok_hl[:, 1, c, cols], hT[:, c], tok_hl[:, 0, c, cols]).then_inc(s_hl, 1)

            def keep_logits(g):
                dve.wait_ge(s_rl, g + 1)
                nc.vector.tensor_copy(logits[:, BG * g:BG * g + BG],
                                      LOGITS[g][:, 0:BG * EG].rearrange("p (b e) -> p b e", b=BG)).then_inc(s_log, 1)

            for g in range(TG):
                if g >= 1:
                    own = make_h(g - 1, own)
                for c in range(F1):
                    dve.wait_ge(s_fh, F1 * g + c + 1)
                    low_half(hid_hl[:, c % 4, 1], gel[:, c % 2], hid_hl[:, c % 4, 0]).then_inc(s_fl, 1)
                    if g + 1 < TG:
                        if c == 0:
                            gated_attention(g + 1)
                        if c == 1:
                            residual(g + 1)
                        if c == 3:
                            own = statistics2(g + 1, own)
                        if c == 4:
                            normalise2(g + 1)
                        if c == 7:
                            low2(g + 1)
                    if g >= 1:
                        if c == 2:
                            keep_logits(g - 1)
                        if c == 5:
                            low_h(g - 1)
                    if g == TG - 1:
                        if c == 3:
                            dve.wait_ge(s_wg, 1)
                            own = shift_logits(0, B - BG, own)
                        if c == 4:
                            nc.vector.memset(comb_r.bitcast(f32), 0.0).then_inc(s_czero, 1)

            own = combine_weights(1, 0, B - BG, own)
            own = make_h(TG - 1, own)
            for g in range(TG - 2):
                low_comb(g)
            keep_logits(TG - 1)
            own = shift_logits(B - BG, B, own)
            low_h(TG - 1)
            own = combine_weights(2, B - BG, B, own)
            for g in range(TG - 2, TG):
                low_comb(g)

            def chunk(k0, i):
                dve.wait_ge(s_sil, k0 + (i + 1))
                nc.vector.tensor_tensor(gu[:, i % 2], UP[i % 2][:, :], sil[:, i % 2], ALU.mult).then_inc(s_gu, 1)
                dve.wait_ge(s_gu, k0 + (i + 1))
                nc.vector.tensor_tensor(hw[:, i % 2], COMB[:, :], gu[:, i % 2], ALU.mult).then_inc(s_hw, 1)
                dve.wait_ge(s_hh3, k0 + (i + 1))
                low_half(hid_hl[:, i % 4, 1], hw[:, i % 2], hid_hl[:, i % 4, 0]).then_inc(s_hl3, 1)

            def add_down(u0, u):
                dve.wait_ge(s_d, u0 + (u + 1))
                for c in range(KD):
                    here = acc[:, c, N * (u % TG):N * (u % TG) + N]
                    nc.vector.tensor_tensor(here, DOWN[c][:, :], here, ALU.add).then_inc(s_da, 1)

            dve.wait_ge(s_clr, 2)
            dve.sem_inc(s_da, 1)
            chunk(0, 0)
            with dve.Fori(0, NCG // 2) as it:
                for i in range(2 * TG * CG):
                    chunk(2 * TG * CG * it, i + 1)
                    if i % CG == CG - 1:
                        add_down(2 * TG * it, i // CG)
            k0, u0 = 2 * TG * CG * (NCG // 2), 2 * TG * (NCG // 2)

            def result(g, m):
                dve.wait_ge(s_fT, 2 * g + m + 1)
                if m == 0:
                    dve.wait_ge(s_xf[g % 2], 16 * (g // 2 + 1))
                    if g >= 2:
                        dve.wait_ge(s_out[g % 2], 16)
                nc.vector.tensor_tensor(y_fin[:, g % 2, 2 * m:2 * m + 2],
                                        SPARE[:, :].rearrange("p (b d) -> p b d", b=2),
                                        x_fin[:, g % 2, 2 * m:2 * m + 2], ALU.add).then_inc(s_fin, 1)

            for i in range(TG * CG):
                if i + 1 < TG * CG:
                    chunk(k0, i + 1)
                if i % CG == CG - 1:
                    add_down(u0, i // CG)
                for m in range(2):
                    g, away = divmod(i - FIN_LAG[m], CG)
                    if g >= 0 and away == 0:
                        result(g, m)
            result(TG - 2, 1)
            for m in range(2):
                result(TG - 1, m)

        @block.tensor
        def _(pe):
            def exact(out_ap, stationary, moving, start, stop):
                for i, (s, m) in enumerate(PARTS):
                    last = nc.tensor.matmul(out_ap, stationary(s), moving(m), start=start and i == 0,
                                            stop=stop and i == len(PARTS) - 1)
                return last

            def modulation(first, many):
                pe.wait_ge(s_aw[min(first, 1)], 16)
                for c in range(first, first + many):
                    for k in range(KD):
                        last = nc.tensor.matmul(bank[6 + first // 4 % 2][:, B * (c - first):B * (c - first + 1)],
                                                ada_w_sb[:, k, P * c:P * c + P], cond_sb[:, k],
                                                start=k == 0, stop=k == KD - 1)
                last.then_inc(s_ada_mm, 1)

            def turn_tokens(source, target):
                for c in range(KD):
                    for b in range(BG):
                        last = nc.tensor.transpose(target[c][:, T * b:T * b + T], source(b, c), id_sb[:, :])
                return last

            def turn1(g):
                pe.wait_ge(s_xhat, g + 1)
                if g >= 2:
                    pe.wait_ge(s_mod, KD * (g - 1))
                turn_tokens(lambda b, c: xhat1[g % 2][:, b, c * P:c * P + P],
                            bank[2 + 2 * (g % 2):4 + 2 * (g % 2)]).then_inc(s_xT, 1)

            def project(it, j, tile):
                g, r = j % TG, (j % BODY) // TG
                if g == 0 and tile == 0:
                    pe.wait_ge(s_wq, (BODY // TG) * it + (j // TG + 1))
                first = isinstance(it, int) and it == 0 and j == 0
                if tile < 2:
                    if not first:
                        pe.wait_ge(s_vv, n_of(it, j, 2, tile - 1))
                else:
                    pe.wait_ge(s_qk, n_of(it, j, 4, tile - 1))
                if tile < 4:
                    for k in range(KD):
                        last = exact(PROJ[tile % 2][:, :],
                                     lambda s: wqkv_hl[:, r, s, k, tile * DH:tile * DH + DH],
                                     lambda s: tok_hl[:, s, k, N * g:N * g + N], k == 0, k == KD - 1)
                else:
                    for b in range(2):
                        col = N * g + T * (2 * (tile - 4) + b)
                        for k in range(KD):
                            last = exact(PROJ[tile % 2][:, HG * DH * b:HG * DH * (b + 1)],
                                         lambda s: tok_hl[:, s, k, col:col + T],
                                         lambda s: wqkv_hl[:, r, s, k, 2 * HG * DH:3 * HG * DH], k == 0, k == KD - 1)
                last.then_inc(s_pj, 1)

            def scores(it, j, m):
                if m == 0:
                    pe.wait_ge(s_qk, n_of(it, j, 4, 4))
                if not (isinstance(it, int) and it == 0 and j == 0):
                    pe.wait_ge(s_exp, n_of(it, j, 2, m - 1))
                for b in range(2):
                    for h in range(HG):
                        i, col = HG * b + h, T * (2 * m + b)
                        last = nc.tensor.matmul(SC[m][:, i * T:i * T + T], qT[:, j % 2, h, col:col + T],
                                                kT[:, j % 2, h, col:col + T], start=True, stop=True)
                last.then_inc(s_s, 1)

            def turn_probs(it, j, m):
                pe.wait_ge(s_pn, n_of(it, j, 2, m + 1))
                if m == 1 or not (isinstance(it, int) and it == 0 and j == 0):
                    pe.wait_ge(s_pt, n_of(it, j, 2, m))
                for i in range(4):
                    last = nc.tensor.transpose(PT[:, i * T:i * T + T], probs[:, m, i], id_sb[:, :])
                last.then_inc(s_t, 1)

            def values(it, j, m):
                pe.wait_ge(s_pt, n_of(it, j, 2, m + 1))
                if m == 0:
                    pe.wait_ge(s_vv, n_of(it, j, 2, 2))
                if m == 1 or not (isinstance(it, int) and it == 0 and j == 0):
                    pe.wait_ge(s_ol, n_of(it, j, 2, m))
                for b in range(2):
                    for h in range(HG):
                        col = (2 * h + b) * T
                        last = nc.tensor.matmul(OB[:, col:col + T], v_sb[:, j % 2, 2 * m + b, h * DH:h * DH + DH],
                                                probsT[:, m, HG * b + h], start=True, stop=True)
                last.then_inc(s_av, 1)

            def output(it, j):
                g, r = j % TG, (j % BODY) // TG
                if g == 0:
                    pe.wait_ge(s_wo, (BODY // TG) * it + (j // TG + 1))
                pe.wait_ge(s_ol, n_of(it, j, 2, 2))
                for c in range(KD):
                    if not (isinstance(it, int) and it == 0 and j == 0):
                        pe.wait_ge(s_acc, n_of(it, j, 2, c - 1) if c else n_of(it, j, 2, -1))
                    for h in range(HG):
                        last = exact(OP[c][:, :], lambda s: wo_hl[:, r, s, h, c * P:c * P + P],
                                     lambda s: o_hl[:, s, h, :], h == 0, h == HG - 1)
                    last.then_inc(s_op, 1)

            def first_half(it, j, more):
                scores(it, j, 0)
                if more:
                    project(it, j + 1, 0)
                scores(it, j, 1)

            def second_half(it, j, more):
                if more:
                    project(it, j + 1, 1)
                turn_probs(it, j, 0)
                if more:
                    project(it, j + 1, 2)
                values(it, j, 0)
                if more:
                    project(it, j + 1, 3)
                turn_probs(it, j, 1)
                if more:
                    project(it, j + 1, 4)
                values(it, j, 1)
                if more:
                    project(it, j + 1, 5)

            pe.wait_ge(s_load, 48)
            modulation(0, 4)
            turn1(0)
            turn1(1)
            pe.wait_ge(s_x1l, KD)
            for tile in range(4):
                project(0, 0, tile)
            turn1(2)
            for tile in range(4, 6):
                project(0, 0, tile)
            turn1(3)
            modulation(4, 8)
            pe.wait_ge(s_x1l, KD * TG)
            first_half(0, 0, True)
            second_half(0, 0, True)
            first_half(0, 1, True)
            output(0, 0)
            with pe.Fori(0, NHG // 2 - 1) as it:
                for j in range(1, BODY + 1):
                    second_half(it, j, True)
                    first_half(it, j + 1, True)
                    output(it, j)
            def turn_x(g):
                pe.wait_ge(s_x2in, 16 * (g + 1))
                if g == 0:
                    pe.wait_ge(s_vv, 2 * UNITS)
                elif g == 1:
                    pe.wait_ge(s_exp, 2 * UNITS)
                else:
                    pe.wait_ge(s_mod, KD * (TG + g))
                turn_tokens(lambda b, c: x_tok2[:, b, c * P:c * P + P], bank[0:2] if g == 0 else bank[2:4])\
                    .then_inc(s_xt2, 1)

            def turn_y(g):
                pe.wait_ge(s_y, KD * (g + 1))
                if g == 1:
                    pe.wait_ge(s_ol, 2 * UNITS)
                if g >= 2:
                    pe.wait_ge(s_log, g - 1)
                for b in range(BG):
                    for c in range(KD):
                        col = D * (b % 2) + P * c
                        last = nc.tensor.transpose(bank[b // 2 if g == 0 else 4 + b // 2][:, col:col + P],
                                                   yT[g % 2][:, c, T * b:T * b + T], id_sb[:, :])
                last.then_inc(s_yt, 1)

            def turn_xhat(g):
                pe.wait_ge(s_xhat, TG + g + 1)
                turn_tokens(lambda b, c: xhat2[:, b, c * P:c * P + P], bank[0:2] if g == 0 else bank[2:4])\
                    .then_inc(s_xT, 1)

            it = NHG // 2 - 1
            for j in range(1, BODY - 1):
                second_half(it, j, True)
                first_half(it, j + 1, j + 1 < BODY - 1)
                if j == BODY - 2:
                    turn_x(0)
                output(it, j)
            j = BODY - 1
            turn_probs(it, j, 0)
            values(it, j, 0)
            turn_probs(it, j, 1)
            turn_y(0)
            values(it, j, 1)
            output(it, j)
            turn_xhat(0)

            def route(g):
                pe.wait_ge(s_h, KD * (g + 1))
                for b in range(BG):
                    for c in range(KD):
                        last = nc.tensor.matmul(LOGITS[g][:, EG * b:EG * b + EG], hT[:, c, T * b:T * b + T],
                                                router_sb[:, c], start=c == 0, stop=c == KD - 1)
                last.then_inc(s_rl, 1)

            pe.wait_ge(s_w12, 2)
            pe.wait_ge(s_rw, 16)
            pe.wait_ge(s_acc, KD * UNITS)
            for g in range(TG):
                pe.wait_ge(s_x1l, KD * (TG + g + 1))

                def up(c):
                    k = F1 * g + c
                    if k >= 2:
                        pe.wait_ge(s_gel, k - 1)
                    for s in range(KD):
                        last = exact(bank[c % 2][:, :], lambda i: w1_hl[:, i, s, c * P:c * P + P],
                                     lambda i: x2_hl[:, g % 2, i, s], s == 0, s == KD - 1)
                    last.then_inc(s_f1, 1)

                up(0)
                up(1)
                if g + 1 < TG:
                    turn_x(g + 1)
                if g >= 1:
                    route(g - 1)
                for c in range(F1):
                    if c + 2 < F1:
                        up(c + 2)
                    pe.wait_ge(s_fl, F1 * g + c + 1)
                    for m in range(KD):
                        last = exact(DOWN[m][:, :], lambda i: w2_hl[:, i, c, m * P:m * P + P],
                                     lambda i: hid_hl[:, c % 4, i], c == 0, c == F1 - 1)
                    if g + 1 < TG:
                        if c == 2:
                            turn_y(g + 1)
                        if c == 5:
                            turn_xhat(g + 1)
                last.then_inc(s_f2, 1)

            def gate_up(k0, g0, i):
                r, g, c = (i // (TG * CG)) % 2, (i // CG) % TG, i % CG
                if i % (TG * CG) == 0:
                    pe.wait_ge(s_wg, g0 + (i // (TG * CG) + 1))
                later = not (isinstance(k0, int) and k0 + i < 2)
                if later:
                    pe.wait_ge(s_sil, k0 + (i - 1))
                for o, banks in enumerate((GATE, UP)):
                    if o == 1 and later:
                        pe.wait_ge(s_gu, k0 + (i - 1))
                    for k in range(KD):
                        exact(banks[i % 2][:, :], lambda s: wgu_hl[r][:, s, k, c, o],
                              lambda s: tok_hl[:, s, k, N * g:N * g + N], k == 0, k == KD - 1)

            def combine(k0, i):
                r, g, c = (i // (TG * CG)) % 2, (i // CG) % TG, i % CG
                if i > 0:
                    pe.wait_ge(s_hw, k0 + i)
                nc.tensor.matmul(COMB[:, :], sel_r[r][:, c], comb_r[0:SELK, N * g:N * g + N],
                                 start=True, stop=True).then_inc(s_g, 1)

            def down(k0, u0, i):
                r, c = (i // (TG * CG)) % 2, i % CG
                pe.wait_ge(s_hl3, k0 + (i + 1))
                if c == 0:
                    pe.wait_ge(s_da, KD * u0 + (KD * (i // CG) + 1))
                for m in range(KD):
                    last = exact(DOWN[m][:, :], lambda s: wd_hl[r][:, s, c, m * P:m * P + P],
                                 lambda s: hid_hl[:, i % 4, s], c == 0, c == CG - 1)
                if c == CG - 1:
                    last.then_inc(s_d, 1)

            def turn_comb(g):
                if g >= 2:
                    pe.wait_ge(s_cl, g - 1)
                for b in range(BG):
                    last = nc.tensor.transpose(bank[4 + g % 2][0:EG, T * b:T * b + T], comb[:, BG * g + b], id_sb[:, :])
                last.then_inc(s_cT, 1)

            pe.wait_ge(s_hl, KD)
            gate_up(0, 0, 0)
            pe.wait_ge(s_comb, 1)
            turn_comb(0)
            turn_comb(1)
            route(TG - 1)
            gate_up(0, 0, 1)
            turn_comb(2)
            pe.wait_ge(s_comb, 2)
            turn_comb(3)
            pe.wait_ge(s_cl, TG)
            pe.wait_ge(s_log, TG)
            pe.wait_ge(s_hl, KD * TG)
            for i in range(LAG):
                combine(0, i)
            body = 2 * TG * CG
            with pe.Fori(0, NCG // 2) as it:
                for i in range(body):
                    gate_up(body * it, 2 * it, i + LAG)
                    combine(body * it, i + LAG)
                    down(body * it, 2 * TG * it, i)
            k0, g0 = body * (NCG // 2), 2 * (NCG // 2)

            def turn_result(g, m):
                pe.wait_ge(s_da, KD * (TG * (NCG - 1) + g + 1) + 1)
                if g + m > 0:
                    pe.wait_ge(s_fin, 2 * g + m)
                for b in range(2):
                    for c in range(KD):
                        tok = N * g + T * (2 * m + b)
                        last = nc.tensor.transpose(SPARE[:, D * b + P * c:D * b + P * c + P], acc[:, c, tok:tok + T],
                                                   id_sb[:, :])
                last.then_inc(s_fT, 1)

            for i in range(TG * CG):
                if i + LAG < TG * CG:
                    gate_up(k0, g0, i + LAG)
                    combine(k0, i + LAG)
                down(k0, g0 * TG, i)
                for m in range(2):
                    g, away = divmod(i - FIN_LAG[m], CG)
                    if g >= 0 and away == 0:
                        turn_result(g, m)
            turn_result(TG - 2, 1)
            for m in range(2):
                turn_result(TG - 1, m)


def kernel(x, cond_2048, L0_cond_ada_w, L0_cond_ada_b, L0_cond_qkv_w, L0_cond_qkv_b, L0_cond_out_w, L0_cond_out_b,
           L0_cond_ffn_w1, L0_cond_ffn_b1, L0_cond_ffn_w2, L0_cond_ffn_b2, L0_ffn_router_w, L0_ffn_w_gate,
           L0_ffn_w_up, L0_ffn_w_down, L0_ffn_sh_gate, L0_ffn_sh_up, L0_ffn_sh_down, L0_ffn_sh_gate_w):
    import numpy as np
    import concourse.bacc as bacc
    from concourse.bass_utils import run_bass_kernel_spmd

    def a(v):
        return np.asarray(v)

    def by_slice(w):
        k, n = w.shape
        return w.reshape(k // P, P, n).transpose(1, 0, 2)

    def columns(b):
        return a(b).reshape(-1, P).T

    def hidden(experts, shared, axis):
        pad = np.zeros((CH * P - HID, D), np.float32)
        e = a(experts).transpose(1, 0, 2).reshape(D, E * I_MOE).T if axis == 2 else a(experts).reshape(E * I_MOE, D)
        s = a(shared).T if axis == 2 else a(shared)
        return np.concatenate([e, s, pad], 0)

    qkv = a(L0_cond_qkv_w).reshape(KD, P, 3, NHG, HG * DH).transpose(3, 1, 0, 2, 4)
    qkv_b = a(L0_cond_qkv_b).reshape(3, NHG, HG, DH)
    gate = hidden(L0_ffn_w_gate, L0_ffn_sh_gate, 2).reshape(NCG, CG, P, KD, P)
    up = hidden(L0_ffn_w_up, L0_ffn_sh_up, 2).reshape(NCG, CG, P, KD, P)
    gu = np.stack([gate, up], 0).transpose(1, 5, 4, 2, 0, 3)
    down = hidden(L0_ffn_w_down, L0_ffn_sh_down, 1).reshape(NCG, CG, P, D).transpose(0, 2, 1, 3)
    sel = np.zeros((SELK, CH * P), np.float32)
    for row in range(HID):
        e = min(row // I_MOE, E)
        sel[e, row] = sel[32 + e, row] = 1.0
    ins = {
        "x": a(x).reshape(B * T, D),
        "condT": a(cond_2048).T.reshape(KD, P, B).transpose(1, 0, 2),
        "ada_w": by_slice(a(L0_cond_ada_w)),
        "bias": np.concatenate([columns(L0_cond_ada_b), columns(L0_cond_out_b), columns(L0_cond_ffn_b1),
                                columns(L0_cond_ffn_b2)], 1),
        "bqk": qkv_b[0:2].transpose(1, 3, 0, 2).reshape(NHG, DH, 2 * HG),
        "bv": qkv_b[2].reshape(NHG, 1, HG * DH),
        "wqkv": qkv.reshape(NHG, P, KD, 3 * HG * DH),
        "wo": a(L0_cond_out_w).reshape(NHG, HG, DH, D).transpose(0, 2, 1, 3),
        "w1": by_slice(a(L0_cond_ffn_w1)),
        "w2": by_slice(a(L0_cond_ffn_w2)),
        "router": by_slice(np.concatenate([a(L0_ffn_router_w).T, a(L0_ffn_sh_gate_w)], 1)),
        "wgu": gu.reshape(NCG, P, KD * CG * 2 * P),
        "wd": down.reshape(NCG, P, CG * D),
        "sel": sel.reshape(SELK, NCG, CG * P).transpose(1, 0, 2),
        "ident": np.eye(P, dtype=np.float32),
    }
    nc = bacc.Bacc("TRN2", target_bir_lowering=False, num_devices=1)
    arrays, args = {}, []
    for name, v in ins.items():
        v = np.ascontiguousarray(v)
        arrays[f"in_{name}"] = v
        args.append(nc.dram_tensor(f"in_{name}", v.shape, mybir.dt.from_np(v.dtype), kind="ExternalInput").ap())
    args.append(nc.dram_tensor("out_y", (B * T, D), mybir.dt.float32, kind="ExternalOutput").ap())
    adaln_moe_kernel(nc, *args)
    r = run_bass_kernel_spmd(nc, [arrays], core_ids=[0])
    return r.results[0]["out_y"].reshape(B, T, D)
```

```python
import concourse.bass as bass
from concourse import mybir
from contextlib import ExitStack

B, T, D = 16, 128, 256
H, DH = 16, 128
MLP = 1024
E, TOPK, I_MOE, I_SH = 16, 4, 176, 704
P = 128
KD = D // P
N = 512
TG = B * T // N
BG = N // T
HG = 2
NHG = H // HG
UNITS = NHG * TG
BODY = 2 * TG
SCALE = DH ** -0.5
LN_EPS = 1e-6
F1 = MLP // P
HID = E * I_MOE + I_SH
CH = -(-HID // P)
CG = 4
NCG = CH // CG
KINDS = 3
PAIR_KINDS = (0, 0, 1, 1, 0, 1, 2, 2)
EK = 8
RK = P // EK
EG = E + 1
SELK = 32 + EG
LAG = 2
AHEAD = CG
FIN_LAG = (CG + 2, CG + 4)


def adaln_moe_kernel(nc, x, condT, ada_w, bias, bqk, bv, wqkv, wo, w1, w2, router, wgu, wd, sel, ident, out):
    f32 = mybir.dt.float32
    f32r = mybir.dt.float32r
    ALU = mybir.AluOpType
    ACT = mybir.ActivationFunctionType
    AX = mybir.AxisListType

    ADA_B, OUT_B, B1, B2 = 0, 12, 14, 22
    SHIFT1, SCALE1, GATE1, SHIFT2, SCALE2, GATE2 = 0, 2, 4, 6, 8, 10

    x_pair = x.rearrange("(g b t) d -> g t b d", b=2, t=T)
    out_pair = out.rearrange("(g b t) d -> g t b d", b=2, t=T)
    x_tok_view = x.rearrange("(g b t) d -> g t b d", b=BG, t=T)

    with ExitStack() as ctx:
        def sb(name, shape, dt=f32):
            return ctx.enter_context(nc.sbuf_tensor(name, shape, dt))

        def sem(name):
            return ctx.enter_context(nc.semaphore(name))

        arena_a = sb("arena_a", [P, 6144], f32r)
        arena_b = sb("arena_b", [P, 8192], f32r)
        tok_hl = sb("tok_hl", [P, 2, KD, B * T], f32r)
        x2_area = sb("x2_area", [P, 4096], f32r)
        hid_area = sb("hid_area", [P, 4096], f32r)
        x2_hl = x2_area[:, :].rearrange("p (g s k n) -> p g s k n", g=2, s=2, k=KD)
        hid_hl = hid_area[:, :].rearrange("p (r s n) -> p r s n", r=4, s=2)
        wqkv_hl = arena_a[:, 0:6144].rearrange("p (r s k n) -> p r s k n", r=2, s=2, k=KD)
        wo_hl = x2_area[:, 2048:4096].rearrange("p (r s h n) -> p r s h n", r=2, s=2, h=HG)
        o_hl = hid_area[:, 0:2048].rearrange("p (s h n) -> p s h n", s=2, h=HG)
        w1_hl = arena_b[:, 0:4096].rearrange("p (s k n) -> p s k n", s=2, k=KD)
        w2_hl = arena_b[:, 4096:8192].rearrange("p (s k n) -> p s k n", s=2, k=F1)
        wgu_hl = [a[:, 0:4096].rearrange("p (s k c g n) -> p s k c g n", s=2, k=KD, c=CG, g=2) for a in (arena_a, arena_b)]
        wd_hl = [a[:, 4096:6144].rearrange("p (s c n) -> p s c n", s=2, c=CG) for a in (arena_a, arena_b)]
        sel_r = sb("sel_r", [SELK, KINDS, P], f32r)
        comb_r = x2_area[0:SELK, 0:B * T]

        acc = sb("acc", [P, KD, B * T])
        raw = sb("raw", [P, 4096])
        bv_sb = sb("bv_sb", [P, 2, HG * DH])
        bqk_sb = sb("bqk_sb", [P, 2, 2 * HG])
        work = sb("work", [P, 8192])
        ada_sb = sb("ada_sb", [P, 12, B])
        bias_sb = sb("bias_sb", [P, 24])
        cond_sb = sb("cond_sb", [P, KD, B])
        router_sb = sb("router_sb", [P, KD, EG])
        id_sb = sb("id_sb", [P, P])
        stats = sb("stats", [P, BG, 6])
        mv = sb("mv", [P, 2, BG, 2])
        veps = sb("veps", [P, 2, BG])
        rstd = sb("rstd", [P, 2, BG])
        mhalf = sb("mhalf", [P, BG])
        ones = sb("ones", [P, 1])
        rmax = sb("rmax", [P, 2, BG])
        negm = sb("negm", [P, 2, BG])
        rsum = sb("rsum", [P, 2, BG])
        rinv = sb("rinv", [P, 2, BG])

        ada_w_sb = acc[:, :, 0:1536]
        def slot(where, first, d=D):
            return where[:, first:first + 1024].rearrange("p (b d) -> p b d", d=d)
        x_in = [slot(work, 1024), slot(work, 3072)]
        xhat1 = [slot(work, 6144), slot(work, 7168)]
        mod1 = [slot(work, 5120, N), slot(raw, 2048, N)]
        raw_qkv = [raw[:, r * 2048:r * 2048 + 1536].rearrange("p (k n) -> p k n", k=KD) for r in range(2)]
        raw_o = [raw[:, r * 2048 + 1536:r * 2048 + 2048].rearrange("p (h n) -> p h n", h=HG) for r in range(2)]
        qT = work[:, 0:2048].rearrange("p (r h n) -> p r h n", r=2, h=HG)
        kT = work[:, 2048:4096].rearrange("p (r h n) -> p r h n", r=2, h=HG)
        v_sb = work[:, 4096:6144].rearrange("p (r b n) -> p r b n", r=2, b=BG)
        probs = work[:, 6144:7168].rearrange("p (r j n) -> p r j n", r=2, j=4)
        probsT = work[:, 7168:8192].rearrange("p (r j n) -> p r j n", r=2, j=4)
        raw_w1 = raw[:, 0:2048].rearrange("p (k n) -> p k n", k=KD)
        raw_w2 = raw[:, 2048:4096].rearrange("p (k n) -> p k n", k=F1)
        raw_gu, raw_d = [[a[:, o + f:o + f + w] for a, o in ((work, 4096), (raw, 0))] for f, w in ((0, 2048), (2048, 1024))]
        x_tok2, xhat2, mod2 = slot(raw, 0), slot(raw, 1024), slot(raw, 2048, N)
        yT = [slot(raw, 3072, N), slot(work, 0, N)]
        hT, part, gel = slot(work, 1024, N), slot(work, 2048, N), slot(work, 3072, N)
        def routed(first, many, n):
            return work[:, 4096 + first:4096 + first + many * n].rearrange("p (b e) -> p b e", b=many)
        logits = sb("logits", [P, B, EG])
        shifted, expd, pr, top, rest, comb = (routed(f, B, n) for f, n in
                                              ((0, E), (256, EG), (528, E), (784, 8), (912, E), (1168, EG)))
        r_small = routed(1440, 7, B)
        sil = work[:, 2048:3072].rearrange("p (r n) -> p r n", r=2)
        gu = work[:, 3072:4096].rearrange("p (r n) -> p r n", r=2)
        hw = work[:, 0:1024].rearrange("p (r n) -> p r n", r=2)
        x_fin = work[:, 4096:5120].rearrange("p (r b d) -> p r b d", r=2, d=D)
        y_fin = work[:, 5120:6144].rearrange("p (r b d) -> p r b d", r=2, d=D)
        spread_a = sb("spread_a", [P, 2, TG, N])
        spread_b = work[:, 6144:8192].rearrange("p (g n) -> p g n", g=TG)
        spread = [spread_a[:, 0], spread_a[:, 1], spread_b]
        sel_raw = raw[0:SELK, 0:KINDS * P]

        bank = [ctx.enter_context(nc.psum_tensor(f"bank{i}", [P, N], f32)) for i in range(8)]
        PROJ, SC, PT, OB, OP = bank[0:2], bank[2:4], bank[4], bank[5], bank[6:8]
        GATE, UP, RESULT, DOWN = bank[0:2], bank[2:4], bank[4:6], bank[6:8]

        LOGITS = [bank[4], bank[4], bank[4], bank[6]]

        ROUTER_STEPS = [("turn", 0, 0), ("turn", 1, 0), ("spread", 0, 0), ("spread", 0, 1), ("spread", 1, 0),
                        ("spread", 1, 1), ("turn", 2, 0), ("spread", 0, 2), ("spread", 2, 0), ("spread", 2, 1),
                        ("spread", 1, 2), ("spread", 2, 2), ("turn", 3, 0), ("spread", 3, 0), ("spread", 3, 1),
                        ("spread", 3, 2)]
        NORM_AT = 4

        TURN1 = [bank[2:4], bank[4:6], bank[6:8], bank[4:6]]

        s_const_loaded = sem("s_const_loaded")
        s_ada_w_loaded = [sem("s_ada_w_loaded_0"), sem("s_ada_w_loaded_1")]
        s_router_loaded = sem("s_router_loaded")
        s_x_loaded = [sem("s_x_loaded_0"), sem("s_x_loaded_1")]
        s_heads_loaded = [sem("s_heads_loaded_0"), sem("s_heads_loaded_1")]
        s_w1_loaded = sem("s_w1_loaded")
        s_w2_loaded = sem("s_w2_loaded")
        s_group_loaded = sem("s_group_loaded")
        s_x2_loaded = sem("s_x2_loaded")
        s_xres_loaded = [sem("s_xres_loaded_0"), sem("s_xres_loaded_1")]
        s_stored = [sem("s_stored_0"), sem("s_stored_1")]
        s_pool_step = sem("s_pool_step")
        s_vector_step = sem("s_vector_step")
        s_acc_cleared = sem("s_acc_cleared")
        s_ada_mm = sem("s_ada_mm")
        s_ada = sem("s_ada")
        s_var = sem("s_var")
        s_rstd = sem("s_rstd")
        s_xhat = sem("s_xhat")
        s_xhat_turned = sem("s_xhat_turned")
        s_mod0 = sem("s_mod0")
        s_mod1 = sem("s_mod1")
        s_mod_high = sem("s_mod_high")
        s_mod_low = sem("s_mod_low")
        s_wqkv0_high = sem("s_wqkv0_high")
        s_wqkv_split = sem("s_wqkv_split")
        s_wo_split = sem("s_wo_split")
        s_w12_split = sem("s_w12_split")
        s_wgu_split = sem("s_wgu_split")
        s_group_split = sem("s_group_split")
        s_proj = sem("s_proj")
        s_qk_kept = sem("s_qk_kept")
        s_v_kept = sem("s_v_kept")
        s_scores = sem("s_scores")
        s_negmax = sem("s_negmax")
        s_exp = sem("s_exp")
        s_probs = sem("s_probs")
        s_probs_turned = sem("s_probs_turned")
        s_probsT_kept = sem("s_probsT_kept")
        s_attended = sem("s_attended")
        s_o_high = sem("s_o_high")
        s_o_low = sem("s_o_low")
        s_outproj = sem("s_outproj")
        s_acc_added = sem("s_acc_added")
        s_gated = sem("s_gated")
        s_x_turned = sem("s_x_turned")
        s_y = sem("s_y")
        s_y_turned = sem("s_y_turned")
        s_ff_up = sem("s_ff_up")
        s_gelu = sem("s_gelu")
        s_ff_high = sem("s_ff_high")
        s_ff_low = sem("s_ff_low")
        s_ff_down = sem("s_ff_down")
        s_h = sem("s_h")
        s_h_high = sem("s_h_high")
        s_h_low = sem("s_h_low")
        s_router_mm = sem("s_router_mm")
        s_logits_kept = sem("s_logits_kept")
        s_shifted = sem("s_shifted")
        s_router_exp = sem("s_router_exp")
        s_comb = sem("s_comb")
        s_comb_turned = sem("s_comb_turned")
        s_comb_high = sem("s_comb_high")
        s_comb_low = sem("s_comb_low")
        s_comb_zero = sem("s_comb_zero")
        s_sel_kept = sem("s_sel_kept")
        s_spread_mm = sem("s_spread_mm")
        s_spread_kept = sem("s_spread_kept")
        s_gate_up = [sem("s_gate"), sem("s_up")]
        s_silu = sem("s_silu")
        s_gated_up = sem("s_gated_up")
        s_weighted = sem("s_weighted")
        s_hidden_high = sem("s_hidden_high")
        s_hidden_low = sem("s_hidden_low")
        s_down = sem("s_down")
        s_down_added = sem("s_down_added")
        s_result_turned = sem("s_result_turned")
        s_result = sem("s_result")

        PARTS = ((0, 0), (0, 1), (1, 0))

        block = ctx.enter_context(nc.Block())

        def flat(ap):
            dims = " ".join("abcd"[:len(ap.shape) - 1])
            return ap.rearrange(f"p {dims} -> p ({dims})")

        def split(eng, halves, whole, done, own):
            hi, lo, whole = flat(halves[:, 0]), flat(halves[:, 1]), flat(whole)
            eng.tensor_tensor(hi, whole, ones[:, 0:1].to_broadcast(whole.shape), ALU.mult).then_inc(s_pool_step, 1)
            eng.wait_ge(s_pool_step, own)
            eng.tensor_tensor(lo, whole, hi.bitcast(f32), ALU.subtract).then_inc(done, 1)

        @block.sync
        def _(sp):
            def load_x(g):
                sp.dma_start(x_in[g % 2], x_tok_view[g]).then_inc(s_x_loaded[g % 2], 16)

            load_x(0)
            sp.dma_start(id_sb[:, :], ident).then_inc(s_const_loaded, 16)
            sp.dma_start(cond_sb[:, :, :], condT).then_inc(s_const_loaded, 16)
            sp.dma_start(bias_sb[:, :], bias).then_inc(s_const_loaded, 16)
            sp.dma_start(ada_w_sb[:, :, 0:512], ada_w[:, :, 0:512]).then_inc(s_ada_w_loaded[0], 16)

            def load_heads(hg, r):
                sp.dma_start(raw_qkv[r], wqkv[hg]).then_inc(s_heads_loaded[r], 16)
                sp.dma_start(raw_o[r], wo[hg]).then_inc(s_heads_loaded[r], 16)
                sp.dma_start(bqk_sb[:, r], bqk[hg]).then_inc(s_heads_loaded[r], 16)
                sp.dma_start(bv_sb[:, r], bv[hg].to_broadcast([P, HG * DH])).then_inc(s_heads_loaded[r], 16)

            def load_group(g, r=1):
                sp.dma_start(raw_gu[r], wgu[g]).then_inc(s_group_loaded, 16)
                sp.dma_start(raw_d[r], wd[g]).then_inc(s_group_loaded, 16)

            load_heads(0, 0)
            load_x(1)
            sp.dma_start(ada_w_sb[:, :, 512:1536], ada_w[:, :, 512:1536]).then_inc(s_ada_w_loaded[1], 16)
            for g in range(2, TG):
                sp.wait_ge(s_xhat, g - 1)
                load_x(g)
            sp.wait_ge(s_mod_low, KD * TG)
            load_heads(1, 1)
            sp.dma_start(router_sb[:, :, :], router).then_inc(s_router_loaded, 16)
            with sp.Fori(1, NHG // 2) as it:
                for r in range(2):
                    sp.wait_ge(s_wo_split, 2 * it + (r - 1))
                    sp.wait_ge(s_v_kept, 16 * it + (8 * r - 8))
                    load_heads(2 * it + r, r)
            sp.wait_ge(s_wo_split, NHG)
            sp.dma_start(raw_w1, w1).then_inc(s_w1_loaded, 16)
            sp.dma_start(raw_w2, w2).then_inc(s_w2_loaded, 16)
            sp.wait_ge(s_w12_split, 2)
            sp.dma_start(x_tok2, x_tok_view[0]).then_inc(s_x2_loaded, 16)
            for g in range(1, TG):
                sp.wait_ge(s_x_turned, g)
                sp.dma_start(x_tok2, x_tok_view[g]).then_inc(s_x2_loaded, 16)
                if g == 1:
                    sp.wait_ge(s_acc_added, KD * UNITS)
                    load_group(0, 0)
            sp.wait_ge(s_x_turned, TG)
            sp.dma_start(sel_raw, sel).then_inc(s_router_loaded, 16)
            sp.wait_ge(s_sel_kept, 1)
            sp.wait_ge(s_h, KD * TG)
            load_group(1)
            with sp.Fori(2, NCG) as g:
                sp.wait_ge(s_group_split, g)
                load_group(g)
            sp.wait_ge(s_comb_turned, TG)
            for q in range(B // 2):
                if q >= 2:
                    sp.wait_ge(s_result, q - 1)
                sp.dma_start(x_fin[:, q % 2], x_pair[q]).then_inc(s_xres_loaded[q % 2], 16)
                if q >= 1:
                    sp.wait_ge(s_result, q)
                    sp.dma_start(out_pair[q - 1], y_fin[:, (q - 1) % 2]).then_inc(s_stored[(q - 1) % 2], 16)
            sp.wait_ge(s_result, B // 2)
            sp.dma_start(out_pair[B // 2 - 1], y_fin[:, 1]).then_inc(s_stored[1], 16)
            for stored in s_stored:
                sp.wait_ge(stored, 16 * B // 4)

        def split_group(eng, r, own, staged=1):
            split(eng, wgu_hl[r], raw_gu[staged].rearrange("p (k c g n) -> p k c g n", k=KD, c=CG, g=2), s_wgu_split, own)
            split(eng, wd_hl[r], raw_d[staged].rearrange("p (c n) -> p c n", c=CG), s_group_split, own + 1)

        @block.gpsimd
        def _(pool):
            pool.memset(mhalf[:, :], -0.5).then_inc(s_pool_step, 1)
            pool.memset(ones[:, :], 1.0).then_inc(s_pool_step, 1)
            own = 2

            def inverse_root(g, r, own):
                pool.wait_ge(s_var, g + 1)
                pool.tensor_scalar(veps[:, r], mv[:, r, :, 1], LN_EPS, None, ALU.add).then_inc(s_pool_step, 1)
                pool.wait_ge(s_pool_step, own + 1)
                pool.tensor_tensor(rstd[:, r], veps[:, r], mhalf[:, :], ALU.pow).then_inc(s_rstd, 1)
                return own + 1

            for g in range(TG):
                if g >= 2:
                    pool.wait_ge(s_xhat, g - 1)
                own = inverse_root(g, g % 2, own)
            pool.wait_ge(s_heads_loaded[0], 64)
            split(pool, wo_hl[:, 0], raw_o[0], s_wo_split, own + 1)
            pool.wait_ge(s_ada_mm, 2)
            pool.memset(acc[:, :, :], 0.0).then_inc(s_acc_cleared, 1)
            pool.wait_ge(s_heads_loaded[1], 64)
            split(pool, wqkv_hl[:, 1], raw_qkv[1], s_wqkv_split, own + 2)
            split(pool, wo_hl[:, 1], raw_o[1], s_wo_split, own + 3)
            own += 3
            with pool.Fori(1, NHG // 2) as it:
                for r in range(2):
                    pool.wait_ge(s_heads_loaded[r], 64 * it + 64)
                    pool.wait_ge(s_proj, 48 * it + (24 * r - 24))
                    split(pool, wqkv_hl[:, r], raw_qkv[r], s_wqkv_split, 4 * it + (own - 4 + 2 * r + 1))
                    pool.wait_ge(s_outproj, 16 * it + (8 * r - 8))
                    split(pool, wo_hl[:, r], raw_o[r], s_wo_split, 4 * it + (own - 4 + 2 * r + 2))
            own += 4 * (NHG // 2 - 1)
            pool.wait_ge(s_w1_loaded, 16)
            split(pool, w1_hl, raw_w1, s_w12_split, own + 1)
            pool.wait_ge(s_w2_loaded, 16)
            split(pool, w2_hl, raw_w2, s_w12_split, own + 2)
            own += 2
            for g in range(TG):
                own = inverse_root(TG + g, g % 2, own)
                if g == 1:
                    pool.wait_ge(s_group_loaded, 32)
                    split_group(pool, 0, own + 1, staged=0)
                    own += 2
            pool.wait_ge(s_gated, KD * TG)
            pool.memset(acc[:, :, :], 0.0).then_inc(s_acc_cleared, 1)
            pool.wait_ge(s_group_loaded, 64)
            pool.wait_ge(s_ff_down, TG)
            split_group(pool, 1, own + 1)
            own += 2
            with pool.Fori(1, NCG // 2) as it:
                for r in range(2):
                    pool.wait_ge(s_group_loaded, 64 * it + (32 * r + 32))
                    pool.wait_ge(s_down, 8 * it + (4 * r - 4))
                    split_group(pool, r, 4 * it + (own - 4 + 2 * r + 1))
            own += 4 * (NCG // 2 - 1)
            pool.wait_ge(s_group_loaded, 32 * NCG)
            pool.wait_ge(s_down, TG * (NCG - 2))
            split_group(pool, 0, own + 1)

        def n_of(it, j, per, c):
            return per * BODY * it + (per * j + c)

        @block.scalar
        def _(act):
            def modulate(g, turned, target, scale, shift):
                for b in range(BG):
                    at = BG * g + b
                    last = nc.scalar.activation(target[:, 0, b * T:b * T + T], turned[0][:, b * T:b * T + T],
                                                ACT.Identity, scale=ada_sb[:, scale, at:at + 1],
                                                bias=ada_sb[:, shift, at:at + 1])
                last.then_inc(s_mod0, 1)

            def modulate1(g):
                act.wait_ge(s_xhat_turned, g + 1)
                if g >= 2:
                    act.wait_ge(s_mod_low, KD * (g - 1))
                modulate(g, TURN1[g], mod1[g % 2], SCALE1, SHIFT1)

            def high1(g, c):
                act.wait_ge(s_mod0 if c == 0 else s_mod1, g + 1)
                nc.scalar.activation(tok_hl[:, 0, c, N * g:N * g + N], mod1[g % 2][:, c], ACT.Copy).then_inc(s_mod_high, 1)

            def project(it, j, tile):
                act.wait_ge(s_proj, n_of(it, j, 6, tile + 1))
                dst = (qT if tile < HG else kT)[:, j % 2, tile % HG]
                r = (j % BODY) // TG
                nc.scalar.activation(dst, PROJ[tile % 2][:, :], ACT.Identity,
                                     bias=bqk_sb[:, r, tile:tile + 1]).then_inc(s_qk_kept, 1)

            def attend(it, j, more, between=None):
                for m in range(2):
                    act.wait_ge(s_negmax, n_of(it, j, 2, m + 1))
                    for i in range(4):
                        last = nc.scalar.activation(probs[:, m, i], SC[m][:, i * T:i * T + T], ACT.Exp,
                                                    bias=negm[:, m, i:i + 1], scale=SCALE,
                                                    accum_out=rsum[:, m, i:i + 1])
                    last.then_inc(s_exp, 1)
                    if more:
                        project(it, j + 1, m)
                for m in range(2):
                    act.wait_ge(s_probs_turned, n_of(it, j, 2, m + 1))
                    nc.scalar.activation(probsT[:, m], PT[:, :].rearrange("p (i n) -> p i n", i=4), ACT.Copy)\
                        .then_inc(s_probsT_kept, 1)
                    if more:
                        project(it, j + 1, 2 + m)
                    if between:
                        between(m)
                    act.wait_ge(s_attended, n_of(it, j, 2, m + 1))
                    nc.scalar.activation(o_hl[:, 0, :, 256 * m:256 * m + 256],
                                         OB[:, :].rearrange("p (h n) -> p h n", h=HG), ACT.Copy).then_inc(s_o_high, 1)

            act.wait_ge(s_heads_loaded[0], 64)
            nc.scalar.activation(flat(wqkv_hl[:, 0, 0]), flat(raw_qkv[0]), ACT.Copy).then_inc(s_wqkv0_high, 1)
            act.wait_ge(s_ada, 1)
            modulate1(0)
            high1(0, 0)
            high1(0, 1)
            project(0, 0, 0)
            project(0, 0, 1)
            modulate1(1)
            project(0, 0, 2)
            high1(1, 0)
            high1(1, 1)
            project(0, 0, 3)
            modulate1(2)
            high1(2, 0)
            high1(2, 1)
            modulate1(3)
            high1(3, 0)
            high1(3, 1)
            attend(0, 0, True)
            with act.Fori(0, NHG // 2 - 1) as it:
                for j in range(1, BODY + 1):
                    if j == TG - 1:
                        act.wait_ge(s_heads_loaded[1], 64 * it + 64)
                    if j == BODY - 1:
                        act.wait_ge(s_heads_loaded[0], 64 * it + 128)
                    attend(it, j, True)
            def second_norm(g):
                act.wait_ge(s_xhat_turned, TG + g + 1)
                if g >= 1:
                    act.wait_ge(s_mod_low, KD * (TG + g))
                modulate(g, bank[6:8] if g == 0 else bank[2:4], mod2, SCALE2, SHIFT2)

            def second_high(g):
                act.wait_ge(s_mod0, TG + g + 1)
                nc.scalar.activation(x2_hl[:, g % 2, 0, 0], mod2[:, 0], ACT.Copy).then_inc(s_mod_high, 1)
                act.wait_ge(s_mod1, TG + g + 1)
                nc.scalar.activation(x2_hl[:, g % 2, 0, 1], mod2[:, 1], ACT.Copy).then_inc(s_mod_high, 1)

            def high_h(g):
                for c in range(KD):
                    act.wait_ge(s_h, KD * g + c + 1)
                    nc.scalar.activation(tok_hl[:, 0, c, N * g:N * g + N], hT[:, c], ACT.Copy).then_inc(s_h_high, 1)

            def exponentials(part, b0, b1):
                act.wait_ge(s_shifted, part)
                nc.scalar.activation(expd[:, b0:b1, 0:E], shifted[:, b0:b1], ACT.Exp)
                nc.scalar.activation(expd[:, b0:b1, E:EG], logits[:, b0:b1, E:EG], ACT.Exp, scale=-1.0)\
                    .then_inc(s_router_exp, 1)

            def norm_of_first(m):
                if m == 0:
                    second_norm(0)
                else:
                    second_high(0)

            for j in range(1, BODY):
                if j == TG - 1:
                    act.wait_ge(s_heads_loaded[1], 64 * NHG // 2)
                attend(NHG // 2 - 1, j, j < BODY - 1, norm_of_first if j == BODY - 2 else None)
            for g in range(TG):
                for c in range(F1):
                    k = F1 * g + c
                    act.wait_ge(s_ff_up, k + 1)
                    if k >= 2:
                        act.wait_ge(s_ff_low, k - 1)
                    nc.scalar.activation(gel[:, c % 2], bank[c % 2][:, :], ACT.Gelu,
                                         bias=bias_sb[:, B1 + c:B1 + c + 1]).then_inc(s_gelu, 1)
                    act.wait_ge(s_gelu, k + 1)
                    nc.scalar.activation(hid_hl[:, (c + 2) % 4, 0], gel[:, c % 2], ACT.Copy).then_inc(s_ff_high, 1)
                    if g >= 1 and c == 1:
                        high_h(g - 1)
                    if g + 1 < TG:
                        if c == NORM_AT + 2:
                            second_norm(g + 1)
                        if c == F1 - 1:
                            second_high(g + 1)
                    elif c == 4:
                        exponentials(1, 0, B - BG)
            act.wait_ge(s_comb_zero, 1)

            def high_comb(g, i):
                act.wait_ge(s_comb_turned, g + 1)
                nc.scalar.activation(comb_r[0:EG, N * g:N * g + N], bank[4 + i % 2][0:EG, :], ACT.Copy)\
                    .then_inc(s_comb_high, 1)

            def keep_spread(i, n, g, kind):
                act.wait_ge(s_spread_mm, n + 1)
                nc.scalar.activation(spread[kind][:, g], bank[4 + i % 2][:, :], ACT.Copy).then_inc(s_spread_kept, 1)

            def router_steps(first, last):
                for i in range(first, last):
                    what, g, kind = ROUTER_STEPS[i]
                    if what == "turn":
                        high_comb(g, i)
                    else:
                        keep_spread(i, sum(w == "spread" for w, _, _ in ROUTER_STEPS[:i]), g, kind)

            def chunk(k0, i):
                act.wait_ge(s_gate_up[0], k0 + (i + 1))
                nc.scalar.activation(sil[:, i % 2], GATE[i % 2][:, :], ACT.Silu).then_inc(s_silu, 1)
                act.wait_ge(s_weighted, k0 + (i + 1))
                nc.scalar.activation(hid_hl[:, i % 4, 0], hw[:, i % 2], ACT.Copy).then_inc(s_hidden_high, 1)

            router_steps(0, 2)
            high_h(TG - 1)
            router_steps(2, 4)
            exponentials(2, B - BG, B)
            for i, last in enumerate((6, 8, 11, 14, 16)):
                chunk(0, i)
                router_steps((4, 6, 8, 11, 14)[i], last)
            with act.Fori(0, NCG // 2) as it:
                for i in range(AHEAD + 1, AHEAD + 1 + 2 * TG * CG):
                    chunk(2 * TG * CG * it, i)
            for i in range(AHEAD + 1, TG * CG):
                chunk(2 * TG * CG * (NCG // 2), i)

        @block.vector
        def _(dve):
            own = 0

            def modulation(first, many, own):
                wide = nc.vector.tensor_tensor(
                    ada_sb[:, first:first + many],
                    bank[6 + first // 4 % 2][:, 0:many * B].rearrange("p (c b) -> p c b", b=B),
                    bias_sb[:, ADA_B + first:ADA_B + first + many].unsqueeze(2).to_broadcast([P, many, B]), ALU.add)
                wide.then_inc(s_vector_step, 1)
                dve.wait_ge(s_vector_step, own + 1)
                c = SCALE1 if first == 0 else SCALE2
                nc.vector.tensor_scalar(ada_sb[:, c:c + KD], ada_sb[:, c:c + KD], 1.0, None, ALU.add)\
                    .then_inc(s_ada, 1)
                return own + 1

            def ada_of(c, g):
                return ada_sb[:, c, BG * g:BG * g + BG].unsqueeze(2).to_broadcast([P, BG, T])

            def by_batch(ap):
                return ap.rearrange("p (b t) -> p b t", b=BG)

            def statistics(source, r, own):
                for b in range(BG):
                    nc.vector.bn_stats(out=stats[:, b], in_=source(b)).then_inc(s_vector_step, 1)
                dve.wait_ge(s_vector_step, own + BG)
                for b in range(BG):
                    last = nc.vector.bn_aggr(out=mv[:, r, b], in_=stats[:, b])
                last.then_inc(s_var, 1)
                return own + BG

            def normalise(g, source, target, r):
                dve.wait_ge(s_rstd, g + 1)
                for b in range(BG):
                    last = nc.vector.tensor_scalar(target[:, b], source(b), mv[:, r, b, 0:1], rstd[:, r, b:b + 1],
                                                   ALU.subtract, ALU.mult)
                last.then_inc(s_xhat, 1)

            def low_half(target, whole, high):
                return nc.vector.tensor_tensor(target, whole, high.bitcast(f32), ALU.subtract)

            def statistics1(g, own):
                dve.wait_ge(s_x_loaded[g % 2], 16 * (g // 2 + 1))
                if g >= 2:
                    dve.wait_ge(s_rstd, g - 1)
                return statistics(lambda b: x_in[g % 2][:, b], g % 2, own)

            def normalise1(g):
                if g >= 2:
                    dve.wait_ge(s_xhat_turned, g - 1)
                normalise(g, lambda b: x_in[g % 2][:, b], xhat1[g % 2], g % 2)

            def modulate_slice(g, turned, target, scale, shift):
                for b in range(BG):
                    at = BG * g + b
                    last = nc.vector.tensor_scalar(target[:, 1, b * T:b * T + T], turned[1][:, b * T:b * T + T],
                                                   ada_sb[:, scale + 1, at:at + 1], ada_sb[:, shift + 1, at:at + 1],
                                                   ALU.mult, ALU.add)
                last.then_inc(s_mod1, 1)

            def modulate1(g):
                dve.wait_ge(s_xhat_turned, g + 1)
                modulate_slice(g, TURN1[g], mod1[g % 2], SCALE1, SHIFT1)

            def low1(g):
                for c in range(KD):
                    dve.wait_ge(s_mod_high, KD * g + c + 1)
                    low_half(tok_hl[:, 1, c, N * g:N * g + N], mod1[g % 2][:, c], tok_hl[:, 0, c, N * g:N * g + N])\
                        .then_inc(s_mod_low, 1)

            own = statistics1(0, own)
            normalise1(0)
            dve.wait_ge(s_const_loaded, 48)
            dve.wait_ge(s_ada_mm, 1)
            own = modulation(0, 4, own)
            dve.wait_ge(s_ada, 1)
            modulate1(0)
            dve.wait_ge(s_wqkv0_high, 1)
            nc.vector.tensor_tensor(flat(wqkv_hl[:, 0, 1]), flat(raw_qkv[0]), flat(wqkv_hl[:, 0, 0]).bitcast(f32),
                                    ALU.subtract).then_inc(s_wqkv_split, 1)
            low1(0)
            own = statistics1(1, own)
            normalise1(1)
            own = statistics1(2, own)
            modulate1(1)
            normalise1(2)
            low1(1)
            own = statistics1(3, own)
            dve.wait_ge(s_ada_mm, 2)
            own = modulation(4, 8, own)
            normalise1(3)

            def head(it, j, base):
                for m in range(2):
                    dve.wait_ge(s_scores, n_of(it, j, 2, m + 1))
                    nc.vector.tensor_reduce(rmax[:, m], SC[m][:, :].rearrange("p (i n) -> p i n", i=4), AX.X, ALU.max)\
                        .then_inc(s_vector_step, 1)
                    dve.wait_ge(s_vector_step, n_of(it, j, 4, base + m + 1))
                    nc.vector.tensor_scalar(negm[:, m], rmax[:, m], -SCALE, None, ALU.mult).then_inc(s_negmax, 1)
                normal(it, j, base, 0)

            def normal(it, j, base, m):
                dve.wait_ge(s_exp, n_of(it, j, 2, m + 1))
                nc.vector.reciprocal(rinv[:, m], rsum[:, m]).then_inc(s_vector_step, 1)
                dve.wait_ge(s_vector_step, n_of(it, j, 4, base + 3 + m))
                nc.vector.tensor_tensor(probs[:, m], probs[:, m], rinv[:, m].unsqueeze(2).to_broadcast([P, 4, T]),
                                        ALU.mult).then_inc(s_probs, 1)

            def add_projection(it, j):
                g = j % TG
                for m in range(KD):
                    dve.wait_ge(s_outproj, n_of(it, j, 2, m + 1))
                    here = acc[:, m, N * g:N * g + N]
                    nc.vector.tensor_tensor(here, OP[m][:, :], here, ALU.add).then_inc(s_acc_added, 1)

            def project_v(it, j, tile):
                dve.wait_ge(s_proj, n_of(it, j, 6, 4 + tile + 1))
                r = (j % BODY) // TG
                nc.vector.tensor_tensor(v_sb[:, j % 2, 2 * tile:2 * tile + 2],
                                        PROJ[tile][:, :].rearrange("p (b n) -> p b n", b=2),
                                        bv_sb[:, r].unsqueeze(1).to_broadcast([P, 2, HG * DH]), ALU.add)\
                    .then_inc(s_v_kept, 1)

            def low_o(it, j, m):
                dve.wait_ge(s_o_high, n_of(it, j, 2, m + 1))
                low_half(o_hl[:, 1, :, 256 * m:256 * m + 256], OB[:, :].rearrange("p (h n) -> p h n", h=HG),
                         o_hl[:, 0, :, 256 * m:256 * m + 256]).then_inc(s_o_low, 1)

            def tail(it, j, base, more):
                normal(it, j, base, 1)
                for m in range(2):
                    low_o(it, j, m)
                    if more:
                        project_v(it, j + 1, m)

            modulate1(2)
            dve.wait_ge(s_heads_loaded[0], 64)
            for tile in range(2):
                project_v(0, 0, tile)
            low1(2)
            modulate1(3)
            base = own
            head(0, 0, base)
            low1(3)
            dve.wait_ge(s_acc_cleared, 1)
            with dve.Fori(0, NHG // 2 - 1) as it:
                for j in range(BODY):
                    if j == TG - 1:
                        dve.wait_ge(s_heads_loaded[1], 64 * it + 64)
                    if j == BODY - 1:
                        dve.wait_ge(s_heads_loaded[0], 64 * it + 128)
                    tail(it, j, base, True)
                    head(it, j + 1, base)
                    add_projection(it, j)
            def gated_attention(g):
                if g >= 2:
                    dve.wait_ge(s_h, KD * (g - 1))
                for c in range(KD):
                    nc.vector.scalar_tensor_tensor(out=by_batch(yT[g % 2][:, c]),
                                                   in0=by_batch(acc[:, c, N * g:N * g + N]),
                                                   scalar=bias_sb[:, OUT_B + c:OUT_B + c + 1], in1=ada_of(GATE1 + c, g),
                                                   op0=ALU.add, op1=ALU.mult).then_inc(s_gated, 1)

            def residual(g):
                dve.wait_ge(s_gated, KD * (g + 1))
                dve.wait_ge(s_x_turned, g + 1)
                for c in range(KD):
                    turned = bank[6 + c if g == 0 else 2 + c]
                    nc.vector.tensor_tensor(yT[g % 2][:, c], turned[:, :], yT[g % 2][:, c], ALU.add).then_inc(s_y, 1)

            def source(g):
                return lambda b: bank[(6 if g == 0 else 4) + b // 2][:, D * (b % 2):D * (b % 2) + D]

            def statistics2(g, own):
                dve.wait_ge(s_y_turned, g + 1)
                return statistics(source(g), g % 2, own)

            def normalise2(g):
                normalise(TG + g, source(g), xhat2, g % 2)

            def modulate2(g):
                dve.wait_ge(s_xhat_turned, TG + g + 1)
                modulate_slice(g, bank[6:8] if g == 0 else bank[2:4], mod2, SCALE2, SHIFT2)

            def low2(g):
                for c in range(KD):
                    dve.wait_ge(s_mod_high, KD * (TG + g) + c + 1)
                    low_half(x2_hl[:, g % 2, 1, c], mod2[:, c], x2_hl[:, g % 2, 0, c]).then_inc(s_mod_low, 1)

            it = NHG // 2 - 1
            for j in range(BODY - 3):
                if j == TG - 1:
                    dve.wait_ge(s_heads_loaded[1], 64 * NHG // 2)
                tail(it, j, base, True)
                head(it, j + 1, base)
                add_projection(it, j)
            dve.wait_ge(s_acc_added, KD * (UNITS - TG + 1))
            dve.wait_ge(s_w12_split, 2)
            gated_attention(0)
            j = BODY - 3
            own += 4 * (UNITS - 2)
            normal(it, j, base, 1)
            residual(0)
            low_o(it, j, 0)
            own = statistics2(0, own)
            base += BG
            project_v(it, j + 1, 0)
            normalise2(0)
            low_o(it, j, 1)
            project_v(it, j + 1, 1)
            head(it, j + 1, base)
            add_projection(it, j)
            j = BODY - 2
            normal(it, j, base, 1)
            modulate2(0)
            low_o(it, j, 0)
            project_v(it, j + 1, 0)
            low_o(it, j, 1)
            low2(0)
            project_v(it, j + 1, 1)
            head(it, j + 1, base)
            add_projection(it, j)
            own += 4 * 2
            tail(it, BODY - 1, base, False)
            add_projection(it, BODY - 1)

            def step(ins, own):
                ins.then_inc(s_vector_step, 1)
                dve.wait_ge(s_vector_step, own + 1)
                return own + 1

            def shift_logits(b0, b1, own):
                dve.wait_ge(s_logits_kept, b1 // BG)
                own = step(nc.vector.tensor_reduce(r_small[:, 0, b0:b1], logits[:, b0:b1, 0:E], AX.X, ALU.max), own)
                nc.vector.tensor_tensor(shifted[:, b0:b1], logits[:, b0:b1, 0:E],
                                        r_small[:, 0, b0:b1].unsqueeze(2).to_broadcast([P, b1 - b0, E]), ALU.subtract)\
                    .then_inc(s_shifted, 1)
                return own

            def small(i, b0, b1):
                return r_small[:, i, b0:b1]

            def along(ap):
                return ap.unsqueeze(2).to_broadcast([P, ap.shape[1], E])

            def probabilities(part, b0, b1, own):
                some = slice(b0, b1)
                dve.wait_ge(s_router_exp, part)
                nc.vector.tensor_reduce(small(1, b0, b1), expd[:, some, 0:E], AX.X, ALU.add).then_inc(s_vector_step, 1)
                own = step(nc.vector.tensor_scalar(small(6, b0, b1), expd[:, some, E], 1.0, None, ALU.add), own + 1)
                nc.vector.reciprocal(comb[:, some, E], small(6, b0, b1)).then_inc(s_vector_step, 1)
                own = step(nc.vector.reciprocal(small(2, b0, b1), small(1, b0, b1)), own + 1)
                nc.vector.tensor_tensor(pr[:, some], expd[:, some, 0:E], along(small(2, b0, b1)), ALU.mult)\
                    .then_inc(s_vector_step, 1)
                return own + 1

            def largest(b0, b1, own):
                some = slice(b0, b1)
                dve.wait_ge(s_vector_step, own)
                for b in range(b0, b1):
                    last = nc.vector.max(out=top[:, b], in_=pr[:, b])
                own = step(last, own)
                own = step(nc.vector.tensor_reduce(small(3, b0, b1), top[:, some, 0:TOPK], AX.X, ALU.add), own)
                nc.vector.memset(top[:, some, TOPK:8], -1.0).then_inc(s_vector_step, 1)
                own = step(nc.vector.tensor_scalar(small(4, b0, b1), small(3, b0, b1), 1e-9, None, ALU.max), own + 1)
                nc.vector.reciprocal(small(5, b0, b1), small(4, b0, b1)).then_inc(s_vector_step, 1)
                return own + 1

            def shares(b0, b1, own):
                some = slice(b0, b1)
                dve.wait_ge(s_vector_step, own)
                for b in range(b0, b1):
                    last = nc.vector.match_replace(out=rest[:, b], in_to_replace=top[:, b], in_values=pr[:, b],
                                                   imm_value=0.0)
                own = step(last, own)
                own = step(nc.vector.tensor_tensor(pr[:, some], pr[:, some], rest[:, some], ALU.subtract), own)
                nc.vector.tensor_tensor(comb[:, some, 0:E], pr[:, some], along(small(5, b0, b1)), ALU.mult)\
                    .then_inc(s_comb, 1)
                return own

            def low_comb(g, i):
                dve.wait_ge(s_comb_high, g + 1)
                low_half(comb_r[32:32 + EG, N * g:N * g + N], bank[4 + i % 2][0:EG, :],
                         comb_r[0:EG, N * g:N * g + N]).then_inc(s_comb_low, 1)

            def make_h(g, own):
                dve.wait_ge(s_ff_down, g + 1)
                for c in range(KD):
                    nc.vector.scalar_tensor_tensor(out=by_batch(part[:, c]), in0=by_batch(DOWN[c][:, :]),
                                                   scalar=bias_sb[:, B2 + c:B2 + c + 1], in1=ada_of(GATE2 + c, g),
                                                   op0=ALU.add, op1=ALU.mult).then_inc(s_vector_step, 1)
                if g >= 1:
                    dve.wait_ge(s_router_mm, g)
                for c in range(KD):
                    dve.wait_ge(s_vector_step, own + c + 1)
                    nc.vector.tensor_tensor(hT[:, c], part[:, c], yT[g % 2][:, c], ALU.add).then_inc(s_h, 1)
                return own + KD

            def low_h(g):
                for c in range(KD):
                    dve.wait_ge(s_h_high, KD * g + c + 1)
                    cols = slice(N * g, N * g + N)
                    low_half(tok_hl[:, 1, c, cols], hT[:, c], tok_hl[:, 0, c, cols]).then_inc(s_h_low, 1)

            def keep_logits(g):
                dve.wait_ge(s_router_mm, g + 1)
                nc.vector.tensor_copy(logits[:, BG * g:BG * g + BG],
                                      LOGITS[g][:, 0:BG * EG].rearrange("p (b e) -> p b e", b=BG)).then_inc(s_logits_kept, 1)

            for g in range(TG):
                if g >= 1:
                    own = make_h(g - 1, own)
                for c in range(F1):
                    dve.wait_ge(s_ff_high, F1 * g + c + 1)
                    low_half(hid_hl[:, (c + 2) % 4, 1], gel[:, c % 2], hid_hl[:, (c + 2) % 4, 0]).then_inc(s_ff_low, 1)
                    if g + 1 < TG:
                        if c == 0:
                            gated_attention(g + 1)
                        if c == 1:
                            residual(g + 1)
                        if c == 2:
                            own = statistics2(g + 1, own)
                        if c == 3:
                            normalise2(g + 1)
                        if c == NORM_AT + 1:
                            modulate2(g + 1)
                        if c == F1 - 1:
                            low2(g + 1)
                    if g >= 1:
                        if c == 1:
                            keep_logits(g - 1)
                        if c == 4:
                            low_h(g - 1)
                    if g == TG - 1:
                        if c == 3:
                            dve.wait_ge(s_group_split, 1)
                            own = shift_logits(0, B - BG, own)
                            nc.vector.memset(comb_r.bitcast(f32), 0.0).then_inc(s_comb_zero, 1)
                        if c == 4:
                            dve.wait_ge(s_router_loaded, 32)
                            nc.vector.tensor_copy(sel_r[:, :, :], sel_raw.rearrange("p (c n) -> p c n", c=KINDS))\
                                .then_inc(s_sel_kept, 1)
                        if c == 5:
                            own = probabilities(1, 0, B - BG, own)
                        if c == 6:
                            own = largest(0, B - BG, own)

            own = shares(0, B - BG, own)
            own = make_h(TG - 1, own)
            turns = [i for i, (what, _, _) in enumerate(ROUTER_STEPS) if what == "turn"]
            for g in range(2):
                low_comb(g, turns[g])
            keep_logits(TG - 1)
            own = shift_logits(B - BG, B, own)
            low_h(TG - 1)

            def chunk(k0, i):
                dve.wait_ge(s_silu, k0 + (i + 1))
                dve.wait_ge(s_gate_up[1], k0 + (i + 1))
                nc.vector.tensor_tensor(gu[:, i % 2], UP[i % 2][:, :], sil[:, i % 2], ALU.mult).then_inc(s_gated_up, 1)
                dve.wait_ge(s_gated_up, k0 + (i + 1))
                weight = spread[PAIR_KINDS[(i // (TG * CG) * CG + i % CG) % len(PAIR_KINDS)]][:, i // CG % TG]
                nc.vector.tensor_tensor(hw[:, i % 2], gu[:, i % 2], weight, ALU.mult).then_inc(s_weighted, 1)
                dve.wait_ge(s_hidden_high, k0 + (i + 1))
                low_half(hid_hl[:, i % 4, 1], hw[:, i % 2], hid_hl[:, i % 4, 0]).then_inc(s_hidden_low, 1)

            def add_down(u0, u):
                dve.wait_ge(s_down, u0 + (u + 1))
                for c in range(KD):
                    here = acc[:, c, N * (u % TG):N * (u % TG) + N]
                    nc.vector.tensor_tensor(here, DOWN[c][:, :], here, ALU.add).then_inc(s_down_added, 1)

            dve.wait_ge(s_acc_cleared, 2)
            dve.sem_inc(s_down_added, 1)
            dve.wait_ge(s_spread_kept, 1)
            chunk(0, 0)
            own = probabilities(2, B - BG, B, own)
            chunk(0, 1)
            low_comb(2, turns[2])
            own = largest(B - BG, B, own)
            dve.wait_ge(s_spread_kept, 2)
            chunk(0, 2)
            own = shares(B - BG, B, own)
            chunk(0, 3)
            low_comb(3, turns[3])
            dve.wait_ge(s_spread_kept, 3)
            chunk(0, AHEAD)
            add_down(0, 0)
            dve.wait_ge(s_spread_kept, KINDS * TG)
            with dve.Fori(0, NCG // 2) as it:
                for i in range(AHEAD, AHEAD + 2 * TG * CG):
                    chunk(2 * TG * CG * it, i + 1)
                    if i % CG == CG - 1:
                        add_down(2 * TG * it, i // CG)
            k0, u0 = 2 * TG * CG * (NCG // 2), 2 * TG * (NCG // 2)

            def result(g, m):
                q = 2 * g + m
                dve.wait_ge(s_result_turned, q + 1)
                dve.wait_ge(s_xres_loaded[q % 2], 16 * (q // 2 + 1))
                if q >= 2:
                    dve.wait_ge(s_stored[q % 2], 16 * (q // 2))
                nc.vector.tensor_tensor(y_fin[:, q % 2], RESULT[q % 2][:, :].rearrange("p (b d) -> p b d", b=2),
                                        x_fin[:, q % 2], ALU.add).then_inc(s_result, 1)

            for i in range(AHEAD, TG * CG):
                if i + 1 < TG * CG:
                    chunk(k0, i + 1)
                if i % CG == CG - 1:
                    add_down(u0, i // CG)
                for m in range(2):
                    g, away = divmod(i - FIN_LAG[m], CG)
                    if g >= 0 and away == 0:
                        result(g, m)
            result(TG - 2, 1)
            for m in range(2):
                result(TG - 1, m)

        @block.tensor
        def _(pe):
            def exact(out_ap, stationary, moving, start, stop):
                for i, (s, m) in enumerate(PARTS):
                    last = nc.tensor.matmul(out_ap, stationary(s), moving(m), start=start and i == 0,
                                            stop=stop and i == len(PARTS) - 1)
                return last

            def modulation(first, many):
                pe.wait_ge(s_ada_w_loaded[min(first, 1)], 16)
                for c in range(first, first + many):
                    for k in range(KD):
                        last = nc.tensor.matmul(bank[6 + first // 4 % 2][:, B * (c - first):B * (c - first + 1)],
                                                ada_w_sb[:, k, P * c:P * c + P], cond_sb[:, k],
                                                start=k == 0, stop=k == KD - 1)
                last.then_inc(s_ada_mm, 1)

            def turn_tokens(source, target):
                for c in range(KD):
                    for b in range(BG):
                        last = nc.tensor.transpose(target[c][:, T * b:T * b + T], source(b, c), id_sb[:, :])
                return last

            def turn1(g):
                pe.wait_ge(s_xhat, g + 1)
                if g == 2:
                    pe.wait_ge(s_ada, 2)
                if g == 3:
                    pe.wait_ge(s_mod0, 2)
                    pe.wait_ge(s_mod1, 2)
                turn_tokens(lambda b, c: xhat1[g % 2][:, b, c * P:c * P + P], TURN1[g]).then_inc(s_xhat_turned, 1)

            def project(it, j, tile):
                g, r = j % TG, (j % BODY) // TG
                if g == 0 and tile == 0:
                    pe.wait_ge(s_wqkv_split, (BODY // TG) * it + (j // TG + 1))
                first = isinstance(it, int) and it == 0 and j == 0
                if tile < 2:
                    if not first:
                        pe.wait_ge(s_v_kept, n_of(it, j, 2, tile - 1))
                else:
                    pe.wait_ge(s_qk_kept, n_of(it, j, 4, tile - 1))
                if tile < 4:
                    for k in range(KD):
                        last = exact(PROJ[tile % 2][:, :],
                                     lambda s: wqkv_hl[:, r, s, k, tile * DH:tile * DH + DH],
                                     lambda s: tok_hl[:, s, k, N * g:N * g + N], k == 0, k == KD - 1)
                else:
                    for b in range(2):
                        col = N * g + T * (2 * (tile - 4) + b)
                        for k in range(KD):
                            last = exact(PROJ[tile % 2][:, HG * DH * b:HG * DH * (b + 1)],
                                         lambda s: tok_hl[:, s, k, col:col + T],
                                         lambda s: wqkv_hl[:, r, s, k, 2 * HG * DH:3 * HG * DH], k == 0, k == KD - 1)
                last.then_inc(s_proj, 1)

            def scores(it, j, m):
                if m == 0:
                    pe.wait_ge(s_qk_kept, n_of(it, j, 4, 4))
                if not (isinstance(it, int) and it == 0 and j == 0):
                    pe.wait_ge(s_exp, n_of(it, j, 2, m - 1))
                for b in range(2):
                    for h in range(HG):
                        i, col = HG * b + h, T * (2 * m + b)
                        last = nc.tensor.matmul(SC[m][:, i * T:i * T + T], qT[:, j % 2, h, col:col + T],
                                                kT[:, j % 2, h, col:col + T], start=True, stop=True)
                last.then_inc(s_scores, 1)

            def turn_probs(it, j, m):
                pe.wait_ge(s_probs, n_of(it, j, 2, m + 1))
                if m == 1 or not (isinstance(it, int) and it == 0 and j == 0):
                    pe.wait_ge(s_probsT_kept, n_of(it, j, 2, m))
                for i in range(4):
                    last = nc.tensor.transpose(PT[:, i * T:i * T + T], probs[:, m, i], id_sb[:, :])
                last.then_inc(s_probs_turned, 1)

            def values(it, j, m):
                pe.wait_ge(s_probsT_kept, n_of(it, j, 2, m + 1))
                if m == 0:
                    pe.wait_ge(s_v_kept, n_of(it, j, 2, 2))
                if m == 1 or not (isinstance(it, int) and it == 0 and j == 0):
                    pe.wait_ge(s_o_low, n_of(it, j, 2, m))
                for b in range(2):
                    for h in range(HG):
                        col = (2 * h + b) * T
                        last = nc.tensor.matmul(OB[:, col:col + T], v_sb[:, j % 2, 2 * m + b, h * DH:h * DH + DH],
                                                probsT[:, m, HG * b + h], start=True, stop=True)
                last.then_inc(s_attended, 1)

            def output(it, j):
                g, r = j % TG, (j % BODY) // TG
                if g == 0:
                    pe.wait_ge(s_wo_split, (BODY // TG) * it + (j // TG + 1))
                pe.wait_ge(s_o_low, n_of(it, j, 2, 2))
                for c in range(KD):
                    if not (isinstance(it, int) and it == 0 and j == 0):
                        pe.wait_ge(s_acc_added, n_of(it, j, 2, c - 1) if c else n_of(it, j, 2, -1))
                    for h in range(HG):
                        last = exact(OP[c][:, :], lambda s: wo_hl[:, r, s, h, c * P:c * P + P],
                                     lambda s: o_hl[:, s, h, :], h == 0, h == HG - 1)
                    last.then_inc(s_outproj, 1)

            def first_half(it, j, more):
                scores(it, j, 0)
                if more:
                    project(it, j + 1, 0)
                scores(it, j, 1)

            def second_half(it, j, more, early=None, late=None):
                if more:
                    project(it, j + 1, 1)
                if early:
                    early(0)
                turn_probs(it, j, 0)
                if more:
                    project(it, j + 1, 2)
                values(it, j, 0)
                if late:
                    late(0)
                if more:
                    project(it, j + 1, 3)
                turn_probs(it, j, 1)
                if more:
                    project(it, j + 1, 4)
                values(it, j, 1)
                if more:
                    project(it, j + 1, 5)

            pe.wait_ge(s_const_loaded, 48)
            modulation(0, 4)
            turn1(0)
            pe.wait_ge(s_mod_low, KD)
            for tile in range(6):
                project(0, 0, tile)
                if tile == 1:
                    turn1(1)
                if tile == 3:
                    modulation(4, 8)
                if tile == 4:
                    turn1(2)
            turn1(3)
            scores(0, 0, 0)
            pe.wait_ge(s_mod_low, KD * 2)
            project(0, 1, 0)
            scores(0, 0, 1)
            pe.wait_ge(s_mod0, TG)
            pe.wait_ge(s_mod1, TG)
            second_half(0, 0, True)
            scores(0, 1, 0)
            pe.wait_ge(s_mod_low, KD * 3)
            project(0, 2, 0)
            scores(0, 1, 1)
            output(0, 0)
            pe.wait_ge(s_mod_low, KD * TG)
            with pe.Fori(0, NHG // 2 - 1) as it:
                for j in range(1, BODY + 1):
                    second_half(it, j, True)
                    first_half(it, j + 1, True)
                    output(it, j)
            def turn_x(g):
                pe.wait_ge(s_x2_loaded, 16 * (g + 1))
                if g == 0:
                    pe.wait_ge(s_acc_added, KD * (UNITS - 3))
                elif g == 1:
                    pe.wait_ge(s_exp, 2 * UNITS)
                else:
                    pe.wait_ge(s_mod0, TG + g)
                    pe.wait_ge(s_mod1, TG + g)
                turn_tokens(lambda b, c: x_tok2[:, b, c * P:c * P + P], bank[6:8] if g == 0 else bank[2:4])\
                    .then_inc(s_x_turned, 1)

            def turn_y(g):
                pe.wait_ge(s_y, KD * (g + 1))
                if g == 1:
                    pe.wait_ge(s_o_low, 2 * UNITS)
                if g >= 2:
                    pe.wait_ge(s_logits_kept, g - 1)
                for b in range(BG):
                    for c in range(KD):
                        col = D * (b % 2) + P * c
                        last = nc.tensor.transpose(bank[(6 if g == 0 else 4) + b // 2][:, col:col + P],
                                                   yT[g % 2][:, c, T * b:T * b + T], id_sb[:, :])
                last.then_inc(s_y_turned, 1)

            def turn_xhat(g):
                pe.wait_ge(s_xhat, TG + g + 1)
                if g == 0:
                    pe.wait_ge(s_acc_added, KD * (UNITS - 2))
                turn_tokens(lambda b, c: xhat2[:, b, c * P:c * P + P], bank[6:8] if g == 0 else bank[2:4])\
                    .then_inc(s_xhat_turned, 1)

            it = NHG // 2 - 1
            for j in range(1, BODY - 3):
                second_half(it, j, True)
                first_half(it, j + 1, True)
                output(it, j)
            j = BODY - 3
            second_half(it, j, True, turn_x, turn_y)
            first_half(it, j + 1, True)
            pe.wait_ge(s_xhat, TG + 1)
            output(it, j)
            j = BODY - 2
            second_half(it, j, True, turn_xhat)
            first_half(it, j + 1, False)
            pe.wait_ge(s_mod0, TG + 1)
            pe.wait_ge(s_mod1, TG + 1)
            output(it, j)

            def route(g):
                pe.wait_ge(s_h, KD * (g + 1))
                for b in range(BG):
                    for c in range(KD):
                        last = nc.tensor.matmul(LOGITS[g][:, EG * b:EG * b + EG], hT[:, c, T * b:T * b + T],
                                                router_sb[:, c], start=c == 0, stop=c == KD - 1)
                last.then_inc(s_router_mm, 1)

            def up(g, c):
                k = F1 * g + c
                if c == 0:
                    pe.wait_ge(s_mod_low, KD * (TG + g + 1))
                if k >= 2:
                    pe.wait_ge(s_gelu, k - 1)
                for s in range(KD):
                    last = exact(bank[c % 2][:, :], lambda i: w1_hl[:, i, s, c * P:c * P + P],
                                 lambda i: x2_hl[:, g % 2, i, s], s == 0, s == KD - 1)
                last.then_inc(s_ff_up, 1)

            pe.wait_ge(s_w12_split, 2)
            pe.wait_ge(s_router_loaded, 16)
            j = BODY - 1
            turn_probs(it, j, 0)
            up(0, 0)
            values(it, j, 0)
            turn_probs(it, j, 1)
            values(it, j, 1)
            up(0, 1)
            output(it, j)
            for g in range(TG):
                if g >= 1:
                    up(g, 0)
                    up(g, 1)
                if g + 1 < TG:
                    turn_x(g + 1)
                if g >= 1:
                    route(g - 1)
                for c in range(F1):
                    if c + 2 < F1:
                        up(g, c + 2)
                    pe.wait_ge(s_ff_low, F1 * g + c + 1)
                    if g == 0 and c == 0:
                        pe.wait_ge(s_acc_added, KD * UNITS)
                    for m in range(KD):
                        last = exact(DOWN[m][:, :], lambda i: w2_hl[:, i, c, m * P:m * P + P],
                                     lambda i: hid_hl[:, (c + 2) % 4, i], c == 0, c == F1 - 1)
                    if g + 1 < TG:
                        if c == 1:
                            turn_y(g + 1)
                        if c == NORM_AT:
                            turn_xhat(g + 1)
                last.then_inc(s_ff_down, 1)

            def gate_up(k0, g0, i):
                r, g, c = (i // (TG * CG)) % 2, (i // CG) % TG, i % CG
                if i % (TG * CG) == 0:
                    pe.wait_ge(s_group_split, g0 + (i // (TG * CG) + 1))
                later = not (isinstance(k0, int) and k0 + i < 2)
                if later:
                    pe.wait_ge(s_silu, k0 + (i - 1))
                for o, banks in enumerate((GATE, UP)):
                    if o == 1 and later:
                        pe.wait_ge(s_gated_up, k0 + (i - 1))
                    for k in range(KD):
                        last = exact(banks[i % 2][:, :], lambda s: wgu_hl[r][:, s, k, c, o],
                                     lambda s: tok_hl[:, s, k, N * g:N * g + N], k == 0, k == KD - 1)
                    last.then_inc(s_gate_up[o], 1)

            def down(k0, u0, i):
                r, c = (i // (TG * CG)) % 2, i % CG
                pe.wait_ge(s_hidden_low, k0 + (i + 1))
                if c == 0:
                    pe.wait_ge(s_down_added, KD * u0 + (KD * (i // CG) + 1))
                for m in range(KD):
                    last = exact(DOWN[m][:, :], lambda s: wd_hl[r][:, s, c, m * P:m * P + P],
                                 lambda s: hid_hl[:, i % 4, s], c == 0, c == CG - 1)
                if c == CG - 1:
                    last.then_inc(s_down, 1)

            def turn_comb(g, i):
                for b in range(BG):
                    last = nc.tensor.transpose(bank[4 + i % 2][0:EG, T * b:T * b + T], comb[:, BG * g + b], id_sb[:, :])
                last.then_inc(s_comb_turned, 1)

            def spread_comb(g, kind, i):
                pe.wait_ge(s_comb_low, g + 1)
                nc.tensor.matmul(bank[4 + i % 2][:, :], sel_r[:, kind], comb_r[:, N * g:N * g + N],
                                 start=True, stop=True).then_inc(s_spread_mm, 1)

            def router_steps(first, last):
                for i in range(first, last):
                    if i >= 2:
                        before = ROUTER_STEPS[:i - 1]
                        if before[-1][0] == "turn":
                            pe.wait_ge(s_comb_low, sum(w == "turn" for w, _, _ in before))
                        else:
                            pe.wait_ge(s_spread_kept, sum(w == "spread" for w, _, _ in before))
                    what, g, kind = ROUTER_STEPS[i]
                    if what == "turn":
                        turn_comb(g, i)
                    else:
                        spread_comb(g, kind, i)

            pe.wait_ge(s_h_low, KD)
            gate_up(0, 0, 0)
            pe.wait_ge(s_comb, 1)
            pe.wait_ge(s_sel_kept, 1)
            router_steps(0, 2)
            route(TG - 1)
            router_steps(2, 4)
            gate_up(0, 0, 1)
            router_steps(4, 6)
            gate_up(0, 0, 2)
            router_steps(6, 7)
            pe.wait_ge(s_logits_kept, TG)
            down(0, 0, 0)
            router_steps(7, 8)
            gate_up(0, 0, 3)
            router_steps(8, 10)
            down(0, 0, 1)
            router_steps(10, 11)
            gate_up(0, 0, 4)
            router_steps(11, 12)
            pe.wait_ge(s_comb, 2)
            router_steps(12, 13)
            down(0, 0, 2)
            router_steps(13, 14)
            gate_up(0, 0, 5)
            router_steps(14, 16)
            down(0, 0, 3)
            pe.wait_ge(s_h_low, KD * TG)
            body = 2 * TG * CG
            with pe.Fori(0, NCG // 2) as it:
                for i in range(AHEAD, AHEAD + body):
                    gate_up(body * it, 2 * it, i + LAG)
                    down(body * it, 2 * TG * it, i)
            k0, g0 = body * (NCG // 2), 2 * (NCG // 2)

            def turn_result(g, m):
                pe.wait_ge(s_down_added, KD * (TG * (NCG - 1) + g + 1) + 1)
                if g > 0:
                    pe.wait_ge(s_result, 2 * g + m - 1)
                for b in range(2):
                    for c in range(KD):
                        tok = N * g + T * (2 * m + b)
                        last = nc.tensor.transpose(RESULT[m][:, D * b + P * c:D * b + P * c + P], acc[:, c, tok:tok + T],
                                                   id_sb[:, :])
                last.then_inc(s_result_turned, 1)

            for i in range(AHEAD, TG * CG):
                if i + LAG < TG * CG:
                    gate_up(k0, g0, i + LAG)
                down(k0, g0 * TG, i)
                for m in range(2):
                    g, away = divmod(i - FIN_LAG[m], CG)
                    if g >= 0 and away == 0:
                        turn_result(g, m)
            turn_result(TG - 2, 1)
            for m in range(2):
                turn_result(TG - 1, m)


def kernel(x, cond_2048, L0_cond_ada_w, L0_cond_ada_b, L0_cond_qkv_w, L0_cond_qkv_b, L0_cond_out_w, L0_cond_out_b,
           L0_cond_ffn_w1, L0_cond_ffn_b1, L0_cond_ffn_w2, L0_cond_ffn_b2, L0_ffn_router_w, L0_ffn_w_gate,
           L0_ffn_w_up, L0_ffn_w_down, L0_ffn_sh_gate, L0_ffn_sh_up, L0_ffn_sh_down, L0_ffn_sh_gate_w):
    import numpy as np
    import concourse.bacc as bacc
    from concourse.bass_utils import run_bass_kernel_spmd

    def a(v):
        return np.asarray(v)

    def by_slice(w):
        k, n = w.shape
        return w.reshape(k // P, P, n).transpose(1, 0, 2)

    def columns(b):
        return a(b).reshape(-1, P).T

    order = PAIR_KINDS * (NCG // 2) + PAIR_KINDS[:CG]

    def hidden(experts, shared, axis):
        e, s = (a(experts).transpose(0, 2, 1), a(shared).T) if axis == 2 else (a(experts), a(shared))
        s = np.concatenate([s, np.zeros((order.count(2) * P - I_SH, D), np.float32)], 0)
        e = e.reshape(E // EK, EK, I_MOE // RK, RK, D).transpose(0, 2, 1, 3, 4).reshape(E // EK, I_MOE // RK, P, D)
        by_kind = [list(e[0]), list(e[1]), list(s.reshape(-1, P, D))]
        return np.stack([by_kind[kind].pop(0) for kind in order], 0)

    qkv = a(L0_cond_qkv_w).reshape(KD, P, 3, NHG, HG * DH).transpose(3, 1, 0, 2, 4)
    qkv_b = a(L0_cond_qkv_b).reshape(3, NHG, HG, DH)
    gate = hidden(L0_ffn_w_gate, L0_ffn_sh_gate, 2).reshape(NCG, CG, P, KD, P)
    up = hidden(L0_ffn_w_up, L0_ffn_sh_up, 2).reshape(NCG, CG, P, KD, P)
    gu = np.stack([gate, up], 0).transpose(1, 5, 4, 2, 0, 3)
    down = hidden(L0_ffn_w_down, L0_ffn_sh_down, 1).reshape(NCG, CG, P, D).transpose(0, 2, 1, 3)
    sel = np.zeros((SELK, KINDS, P), np.float32)
    for kind in range(KINDS):
        for row in range(P):
            e = EK * kind + row // RK if kind < E // EK else E
            sel[e, kind, row] = sel[32 + e, kind, row] = 1.0
    ins = {
        "x": a(x).reshape(B * T, D),
        "condT": a(cond_2048).T.reshape(KD, P, B).transpose(1, 0, 2),
        "ada_w": by_slice(a(L0_cond_ada_w)),
        "bias": np.concatenate([columns(L0_cond_ada_b), columns(L0_cond_out_b), columns(L0_cond_ffn_b1),
                                columns(L0_cond_ffn_b2)], 1),
        "bqk": qkv_b[0:2].transpose(1, 3, 0, 2).reshape(NHG, DH, 2 * HG),
        "bv": qkv_b[2].reshape(NHG, 1, HG * DH),
        "wqkv": qkv.reshape(NHG, P, KD, 3 * HG * DH),
        "wo": a(L0_cond_out_w).reshape(NHG, HG, DH, D).transpose(0, 2, 1, 3),
        "w1": by_slice(a(L0_cond_ffn_w1)),
        "w2": by_slice(a(L0_cond_ffn_w2)),
        "router": by_slice(np.concatenate([a(L0_ffn_router_w).T, a(L0_ffn_sh_gate_w)], 1)),
        "wgu": gu.reshape(NCG, P, KD * CG * 2 * P),
        "wd": down.reshape(NCG, P, CG * D),
        "sel": sel.reshape(SELK, KINDS * P),
        "ident": np.eye(P, dtype=np.float32),
    }
    nc = bacc.Bacc("TRN2", target_bir_lowering=False, num_devices=1)
    arrays, args = {}, []
    for name, v in ins.items():
        v = np.ascontiguousarray(v)
        arrays[f"in_{name}"] = v
        args.append(nc.dram_tensor(f"in_{name}", v.shape, mybir.dt.from_np(v.dtype), kind="ExternalInput").ap())
    args.append(nc.dram_tensor("out_y", (B * T, D), mybir.dt.float32, kind="ExternalOutput").ap())
    adaln_moe_kernel(nc, *args)
    r = run_bass_kernel_spmd(nc, [arrays], core_ids=[0])
    return r.results[0]["out_y"].reshape(B, T, D)
```
